# Optimizing a Trainium2 kernel written in Bass

```python
import numpy as np
import jax
import jax.numpy as jnp

def _softmax(x, axis=-1):
    return jax.nn.softmax(x, axis=axis)

def _gelu(x):
    return jax.nn.gelu(x, approximate=True)

def _silu(x):
    return jax.nn.silu(x)

def _sigmoid(x):
    return jax.nn.sigmoid(x)

def _layernorm(x, axis=-1, eps=1e-05):
    m = jnp.mean(x, axis=axis, keepdims=True)
    v = jnp.var(x, axis=axis, keepdims=True)
    return (x - m) / jnp.sqrt(v + eps)

def _scatter_add(tgt, idx, src, axis=0):
    return tgt.at[idx].add(src)

def _segment_sum(src, seg, n):
    return jax.ops.segment_sum(src, seg, n)
kernel_name = 'mk_recurrent_d1_jaxref_r8_50cd53'

def setup_inputs(seed: int=0):
    np.random.seed(seed)
    _w = jnp.asarray

    def _L0_attn_setup():
        import math
        import jax, jax.numpy as jnp
        import numpy as np
        B, S, D = (4, 256, 128)

        def _complex_proj(x, W, b):
            p = jnp.einsum('bsd,ed->bse', x, W) + b
            p = p.reshape(*x.shape[:-1], x.shape[-1], 2)
            return (p[..., 0], p[..., 1])
        key = jax.random.key(seed)
        ks = jax.random.split(key, 9)
        sd = 1.0 / math.sqrt(D)
        return {'hidden_states': jax.random.normal(ks[0], (B, S, D), jnp.float32), 'Wq': jax.random.normal(ks[1], (2 * D, D), jnp.float32) * sd, 'bq': jax.random.normal(ks[2], (2 * D,), jnp.float32) * 0.01, 'Wk': jax.random.normal(ks[3], (2 * D, D), jnp.float32) * sd, 'bk': jax.random.normal(ks[4], (2 * D,), jnp.float32) * 0.01, 'Wv': jax.random.normal(ks[5], (2 * D, D), jnp.float32) * sd, 'bv': jax.random.normal(ks[6], (2 * D,), jnp.float32) * 0.01, 'Wo': jax.random.normal(ks[7], (D, 2 * D), jnp.float32) * sd, 'bo': jax.random.normal(ks[8], (D,), jnp.float32) * 0.01}
    _L0_attn_in = _L0_attn_setup()

    def _L0_ffn_setup():
        import jax, jax.numpy as jnp
        import numpy as np
        D = 128
        H = 16
        HD = D // H
        E = 32
        ES = 128
        K = 4
        B, S = (2, 128)
        ROPE_BASE = 10000.0

        def _layernorm(x, g, b):
            m = x.mean(-1, keepdims=True)
            v = ((x - m) ** 2).mean(-1, keepdims=True)
            return (x - m) * jax.lax.rsqrt(v + 1e-05) * g + b

        def _forward(src, wq, wk, wv, wp, wo, ln1_g, ln1_b, ln2_g, ln2_b, sel_w, keys, values):
            Bs, Ss, Ds = src.shape
            scale = 1.0 / jnp.sqrt(jnp.array(HD, dtype=src.dtype))
            x = _layernorm(src, ln1_g, ln1_b)
            q = (x @ wq).reshape(Bs, Ss, H, HD)
            k = (x @ wk).reshape(Bs, Ss, H, HD)
            v = (x @ wv).reshape(Bs, Ss, H, HD)
            pos = jnp.arange(Ss - 1, -Ss, -1, dtype=src.dtype)
            inv_freq = 1.0 / ROPE_BASE ** (jnp.arange(0, Ds, 2, dtype=src.dtype) / Ds)
            ang = pos[:, None] * inv_freq[None, :]
            pe = jnp.concatenate([jnp.sin(ang), jnp.cos(ang)], axis=-1)
            p = (pe @ wp).reshape(2 * Ss - 1, H, HD)
            ac = jnp.einsum('bihd,bjhd->bhij', q, k)
            bd_full = jnp.einsum('bihd,phd->bhip', q, p)
            rel = jnp.arange(Ss)[:, None] - jnp.arange(Ss)[None, :] + (Ss - 1)
            bd = bd_full[:, :, jnp.arange(Ss)[:, None], rel]
            att = jax.nn.softmax((ac + bd) * scale, axis=-1)
            attn_out = jnp.einsum('bhij,bjhd->bihd', att, v).reshape(Bs, Ss, Ds) @ wo
            src = src + attn_out
            x2 = _layernorm(src, ln2_g, ln2_b)
            sel = jax.nn.sigmoid(x2 @ sel_w)
            scores, idx = jax.lax.top_k(sel, K)
            gate = (jax.nn.one_hot(idx, E, dtype=sel.dtype) * scores[..., None]).sum(-2)
            h = jax.nn.relu(jnp.einsum('bsd,edh->bseh', x2, keys))
            moe_out = jnp.einsum('bseh,ehd,bse->bsd', h, values, gate)
            return src + moe_out
        key = jax.random.key(seed)
        ks = jax.random.split(key, 10)
        std_scale = np.sqrt(2.0 / 18)
        w_std = std_scale / np.sqrt(D)
        return {'src': jax.random.normal(ks[0], (B, S, D), jnp.float32), 'wq': jax.random.normal(ks[1], (D, H * HD), jnp.float32) * w_std, 'wk': jax.random.normal(ks[2], (D, H * HD), jnp.float32) * w_std, 'wv': jax.random.normal(ks[3], (D, H * HD), jnp.float32) * w_std, 'wp': jax.random.normal(ks[4], (D, H * HD), jnp.float32) * w_std, 'wo': jax.random.normal(ks[5], (H * HD, D), jnp.float32) * w_std, 'ln1_g': jnp.ones((D,), jnp.float32), 'ln1_b': jnp.zeros((D,), jnp.float32), 'ln2_g': jnp.ones((D,), jnp.float32), 'ln2_b': jnp.zeros((D,), jnp.float32), 'sel_w': jax.random.normal(ks[6], (D, E), jnp.float32) / np.sqrt(D), 'keys': jax.random.normal(ks[7], (E, D, ES), jnp.float32) * w_std, 'values': jax.random.normal(ks[8], (E, ES, D), jnp.float32) * (std_scale / np.sqrt(ES))}
    _L0_ffn_in = _L0_ffn_setup()
    _d = {'L0_attn_hidden_states': _L0_attn_in['hidden_states'], 'L0_attn_Wq': _L0_attn_in['Wq'], 'L0_attn_bq': _L0_attn_in['bq'], 'L0_attn_Wk': _L0_attn_in['Wk'], 'L0_attn_bk': _L0_attn_in['bk'], 'L0_attn_Wv': _L0_attn_in['Wv'], 'L0_attn_bv': _L0_attn_in['bv'], 'L0_attn_Wo': _L0_attn_in['Wo'], 'L0_attn_bo': _L0_attn_in['bo'], 'L0_ffn_wq': _L0_ffn_in['wq'], 'L0_ffn_wk': _L0_ffn_in['wk'], 'L0_ffn_wv': _L0_ffn_in['wv'], 'L0_ffn_wp': _L0_ffn_in['wp'], 'L0_ffn_wo': _L0_ffn_in['wo'], 'L0_ffn_ln1_g': _L0_ffn_in['ln1_g'], 'L0_ffn_ln1_b': _L0_ffn_in['ln1_b'], 'L0_ffn_ln2_g': _L0_ffn_in['ln2_g'], 'L0_ffn_ln2_b': _L0_ffn_in['ln2_b'], 'L0_ffn_sel_w': _L0_ffn_in['sel_w'], 'L0_ffn_keys': _L0_ffn_in['keys'], 'L0_ffn_values': _L0_ffn_in['values']}
    _x0 = _d['L0_attn_hidden_states']
    _d['L0_attn_hidden_states'] = jax.random.normal(jax.random.fold_in(jax.random.key(seed), 1), (8, 512, 128), dtype=_x0.dtype)
    del _x0
    return _d

def reference(L0_attn_hidden_states, L0_attn_Wq, L0_attn_bq, L0_attn_Wk, L0_attn_bk, L0_attn_Wv, L0_attn_bv, L0_attn_Wo, L0_attn_bo, L0_ffn_wq, L0_ffn_wk, L0_ffn_wv, L0_ffn_wp, L0_ffn_wo, L0_ffn_ln1_g, L0_ffn_ln1_b, L0_ffn_ln2_g, L0_ffn_ln2_b, L0_ffn_sel_w, L0_ffn_keys, L0_ffn_values):

    def _L0_attn_ref(hidden_states, Wq, bq, Wk, bk, Wv, bv, Wo, bo):
        import math
        import jax, jax.numpy as jnp
        import numpy as np
        B, S, D = (4, 256, 128)

        def _complex_proj(x, W, b):
            p = jnp.einsum('bsd,ed->bse', x, W) + b
            p = p.reshape(*x.shape[:-1], x.shape[-1], 2)
            return (p[..., 0], p[..., 1])
        dim = hidden_states.shape[-1]
        qr, qi = _complex_proj(hidden_states, Wq, bq)
        kr, ki = _complex_proj(hidden_states, Wk, bk)
        vr, vi = _complex_proj(hidden_states, Wv, bv)
        scale = 1.0 / math.sqrt(dim)
        scores = (jnp.einsum('bsd,btd->bst', qr, kr) + jnp.einsum('bsd,btd->bst', qi, ki)) * scale
        w = jax.nn.softmax(scores, axis=-1)
        o_r = jnp.einsum('bst,btd->bsd', w, vr)
        o_i = jnp.einsum('bst,btd->bsd', w, vi)
        out = jnp.stack([o_r, o_i], axis=-1).reshape(*hidden_states.shape[:-1], 2 * dim)
        return jnp.einsum('bse,de->bsd', out, Wo) + bo

    def _L0_ffn_ref(src, wq, wk, wv, wp, wo, ln1_g, ln1_b, ln2_g, ln2_b, sel_w, keys, values):
        import jax, jax.numpy as jnp
        import numpy as np
        D = 128
        H = 16
        HD = D // H
        E = 32
        ES = 128
        K = 4
        B, S = (2, 128)
        ROPE_BASE = 10000.0

        def _layernorm(x, g, b):
            m = x.mean(-1, keepdims=True)
            v = ((x - m) ** 2).mean(-1, keepdims=True)
            return (x - m) * jax.lax.rsqrt(v + 1e-05) * g + b

        def _forward(src, wq, wk, wv, wp, wo, ln1_g, ln1_b, ln2_g, ln2_b, sel_w, keys, values):
            Bs, Ss, Ds = src.shape
            scale = 1.0 / jnp.sqrt(jnp.array(HD, dtype=src.dtype))
            x = _layernorm(src, ln1_g, ln1_b)
            q = (x @ wq).reshape(Bs, Ss, H, HD)
            k = (x @ wk).reshape(Bs, Ss, H, HD)
            v = (x @ wv).reshape(Bs, Ss, H, HD)
            pos = jnp.arange(Ss - 1, -Ss, -1, dtype=src.dtype)
            inv_freq = 1.0 / ROPE_BASE ** (jnp.arange(0, Ds, 2, dtype=src.dtype) / Ds)
            ang = pos[:, None] * inv_freq[None, :]
            pe = jnp.concatenate([jnp.sin(ang), jnp.cos(ang)], axis=-1)
            p = (pe @ wp).reshape(2 * Ss - 1, H, HD)
            ac = jnp.einsum('bihd,bjhd->bhij', q, k)
            bd_full = jnp.einsum('bihd,phd->bhip', q, p)
            rel = jnp.arange(Ss)[:, None] - jnp.arange(Ss)[None, :] + (Ss - 1)
            bd = bd_full[:, :, jnp.arange(Ss)[:, None], rel]
            att = jax.nn.softmax((ac + bd) * scale, axis=-1)
            attn_out = jnp.einsum('bhij,bjhd->bihd', att, v).reshape(Bs, Ss, Ds) @ wo
            src = src + attn_out
            x2 = _layernorm(src, ln2_g, ln2_b)
            sel = jax.nn.sigmoid(x2 @ sel_w)
            scores, idx = jax.lax.top_k(sel, K)
            gate = (jax.nn.one_hot(idx, E, dtype=sel.dtype) * scores[..., None]).sum(-2)
            h = jax.nn.relu(jnp.einsum('bsd,edh->bseh', x2, keys))
            moe_out = jnp.einsum('bseh,ehd,bse->bsd', h, values, gate)
            return src + moe_out
        return _forward(src, wq, wk, wv, wp, wo, ln1_g, ln1_b, ln2_g, ln2_b, sel_w, keys, values)
    x = L0_attn_hidden_states
    xn = _layernorm(x, axis=-1)
    s = _L0_attn_ref(xn, L0_attn_Wq, L0_attn_bq, L0_attn_Wk, L0_attn_bk, L0_attn_Wv, L0_attn_bv, L0_attn_Wo, L0_attn_bo)
    g = _silu(_L0_ffn_ref(xn, L0_ffn_wq, L0_ffn_wk, L0_ffn_wv, L0_ffn_wp, L0_ffn_wo, L0_ffn_ln1_g, L0_ffn_ln1_b, L0_ffn_ln2_g, L0_ffn_ln2_b, L0_ffn_sel_w, L0_ffn_keys, L0_ffn_values))
    x = x + s * g
    return x

_drawn_inputs = setup_inputs


def setup_inputs(seed=0):
    import zlib

    import numpy as np

    out = dict(_drawn_inputs(seed))
    spreads = {'L0_ffn_ln1_g': (1.0, 0.6),
     'L0_ffn_ln1_b': (0.0, 0.8),
     'L0_ffn_ln2_g': (1.0, 0.6),
     'L0_ffn_ln2_b': (0.0, 0.8)}
    factors = {'L0_attn_bq': 8.0,
     'L0_attn_bk': 8.0,
     'L0_attn_bv': 6.788,
     'L0_attn_bo': 8.0,
     'L0_ffn_wq': 8.0,
     'L0_ffn_wk': 8.0,
     'L0_ffn_wv': 8.0,
     'L0_ffn_wp': 8.0,
     'L0_ffn_wo': 8.0,
     'L0_ffn_sel_w': 3.184,
     'L0_ffn_keys': 3.617,
     'L0_ffn_values': 3.003}
    for name, (base, spread) in spreads.items():
        noise = np.random.default_rng([zlib.crc32(name.encode()), seed]).standard_normal(out[name].shape)
        drawn = base * np.exp(spread * noise) if base else spread * noise
        out[name] = jnp.asarray(drawn.astype(out[name].dtype))
    for name, factor in factors.items():
        out[name] = (out[name] * factor).astype(out[name].dtype)
    return out
```

```python
from contextlib import ExitStack

import concourse.bass as bass
from concourse import mybir

F32 = mybir.dt.float32
FR = mybir.dt.float32r
U32 = mybir.dt.uint32
ALU = mybir.AluOpType
ACT = mybir.ActivationFunctionType
X = mybir.AxisListType.X

P = 128
B, S = 8, 512
T = S // P
H, HD = 16, 8
E, TOPK = 32, 4
NF = 59
RF = 2 * NF
RQ = RF + HD
RK = RQ + 1
QH = 4
NQ = H // QH
USLOTS = 3
PSLOTS = 8
EPS = 1e-5
HEAD_SCALE = float(HD) ** -0.5
MAIN_SCALE = float(P) ** -0.5

GUARD_AT = 6
SCORE_AT = 27
NT = H * T
TICKS = SCORE_AT + NT + 10
MAIN_GUARD, MAIN_ROW, MAIN_SCORE, MAIN_OUT = 0, 4, 11, 20


def position_constants():
    import numpy as np

    freq = 1.0 / 10000.0 ** (np.arange(0, P, 2) / P)
    keep = 44
    n = NF - keep
    nodes2 = freq[keep] ** 2 * (1 + np.cos((2 * np.arange(n) + 1) * np.pi / (2 * n))) / 2
    nodes = np.sqrt(nodes2)
    low = freq[keep:]
    lag = np.array([[np.prod([(f * f - nodes2[m]) / (nodes2[k] - nodes2[m]) for m in range(n) if m != k])
                     for f in low] for k in range(n)])
    span = np.zeros((P, 2 * NF))
    for k in range(keep):
        span[k, k] = span[P // 2 + k, NF + k] = 1.0
    span[keep:P // 2, keep:NF] = (lag * low[None, :] / nodes[:, None]).T
    span[P // 2 + keep:, NF + keep:] = lag.T
    f = np.concatenate([freq[:keep], nodes])
    at = f[:, None] * np.arange(S)[None, :]
    sin, cos = np.sin(at), np.cos(at)
    swapped = np.concatenate([span[:, NF:], span[:, :NF]], axis=1)
    f32 = np.float32
    return {
        "c_span": np.concatenate([span, swapped], axis=1).astype(f32),
        "c_cos": np.concatenate([cos, cos]).astype(f32),
        "c_sin": np.concatenate([sin, -sin]).astype(f32),
        "c_key": np.concatenate([sin, cos]).astype(f32),
        "c_ident": np.eye(P, dtype=f32),
        "c_pick": np.concatenate([np.eye(E), np.eye(E)]).astype(f32),
        "c_iota": np.tile(np.arange(E, dtype=f32), (P, TOPK)),
    }


def build(nc, x, Wq, bq, Wk, bk, Wv, bv, Wo, bo, wq, wk, wv, wp, wo, ln1_g, ln1_b, ln2_g, ln2_b,
          sel_w, keys, values, c_span, c_cos, c_sin, c_key, c_ident, c_pick, c_iota, out):
    spill = nc.dram_tensor("spill", (4, P, S), F32, kind="Internal").ap()
    spill_w = nc.dram_tensor("spill_w", (2, P, 2 * RF), F32, kind="Internal").ap()
    spill_row = nc.dram_tensor("spill_row", (NQ, QH * T, P), F32, kind="Internal").ap()
    spill_main = nc.dram_tensor("spill_main", (T, P), F32, kind="Internal").ap()

    with ExitStack() as ctx:
        def sb(name, shape, dt=F32):
            return ctx.enter_context(nc.sbuf_tensor(name, shape, dt))

        def ps(name, shape, dt=F32):
            return ctx.enter_context(nc.psum_tensor(name, shape, dt))

        def sem(name):
            return ctx.enter_context(nc.semaphore(name))

        ident = sb("ident", [P, P])
        prob = sb("prob", [P, PSLOTS, S])
        key_table = prob[0:RF, 0, :]
        halves = [prob[:, 1 + n // 2, (n % 2) * 2 * P:(n % 2 + 1) * 2 * P] for n in range(6)]
        WqA, WkA, WvA, WoT = (v.rearrange("p (c n) -> p c n", c=2) for v in halves[0:4])
        WoA, span = halves[4], halves[5][:, 0:2 * RF]
        wpF, bo_row = prob[:, 4, 0:P], prob[:, 4, P:2 * P]
        biasA = sb("biasA", [P, 3, 2])
        wqk = sb("wqk", [P, P])
        wvo = sb("wvo", [P, P + 1])
        y_bias = sb("y_bias", [P, 1])
        bqbk = sb("bqbk", [P, 1])
        out_bias = sb("out_bias", [P, P])
        wqF, wkF, wvF, woF = (sb(n, [P, P]) for n in ("wqF", "wkF", "wvF", "woF"))
        selF = sb("selF", [P, E])
        lnF = sb("lnF", [P, 4])
        keysF = sb("keysF", [P, E, P])
        valsF = sb("valsF", [P, E, P])
        cosT = sb("cosT", [RF, S])
        sinT = sb("sinT", [RF, S])
        pick32 = sb("pick32", [2 * E, E])
        pick = sb("pick", [2 * E, E], FR)
        iota = sb("iota", [P, TOPK, E])
        w_hi = sb("w_hi", [P, 2 * RF], FR)
        w_lo = sb("w_lo", [P, 2 * RF], FR)
        turn_w = sb("turn_w", [P, NQ, 2 * RF], FR)

        xin = sb("xin", [P, T, P])
        xres = sb("xres", [P, T, P])
        xn = sb("xn", [P, T, P])
        zn = sb("zn", [P, T, P])
        stats = sb("stats", [P, T, 6])
        mv = sb("mv", [P, T, 2])
        carrier = sb("carrier", [P, 1])
        rstd = sb("rstd", [P, T])
        var_eps = sb("var_eps", [P, T])
        eps = sb("eps", [P, T])
        minus_half = sb("minus_half", [P, T])
        xnT = sb("xnT", [P, S])
        xfT = sb("xfT", [P, S])
        yT = sb("yT", [P, S])
        vmain = sb("vmain", [P, T, P + 1])
        cmain = sb("cmain", [P, T])
        turn_q = sb("turn_q", [P, NQ, S], FR)
        vhead = sb("vhead", [P, T, H * (HD + 1) + 32])
        u_hi = sb("u_hi", [P, USLOTS, QH, S], FR)
        u_lo = sb("u_lo", [P, USLOTS, QH, S], FR)
        q_hi, q_lo, k_hi, k_lo = (u_hi[:, USLOTS - 1, n, :] for n in range(4))
        k_hi4 = sb("k_hi4", [P, USLOTS, QH, S], FR)
        k_lo4 = sb("k_lo4", [P, USLOTS, QH, S], FR)
        rot_a = sb("rot_a", [RF, 2, S])
        rot_b = sb("rot_b", [RF, 2, S])
        rowmax = sb("rowmax", [P, 2, QH * T])
        rowmaxT = sb("rowmaxT", [QH * T, 2, P], FR)
        mmax = sb("mmax", [P, 3, T])
        mainrowT = sb("mainrowT", [T, P])
        mainrow = sb("mainrow", [1, S])
        ones_row = sb("ones_row", [1, P])
        smain = sb("smain", [P, T, P])
        rmain = sb("rmain", [P, T])
        oT = sb("oT", [P, S])
        rhead = sb("rhead", [P, T, QH])
        attn = sb("attn", [P, T, H, HD])
        attnT = oT
        src2 = xnT[:, :].rearrange("p (t d) -> p t d", t=T)
        x2T = xfT
        sel = sb("sel", [P, T, E])
        selx = sb("selx", [P, T, E])
        top = sb("top", [P, T, 8])
        topi = sb("topi", [P, T, 8], U32)
        topf = sb("topf", [P, T, 8])
        hit = yT[:, :].rearrange("p (t k e) -> p t k e", t=T, k=TOPK)
        gate = sb("gate", [P, T, E])
        gateT = u_hi[0:2 * E, USLOTS - 1, 0, :]
        hrelu, hgate = prob[:, 0:2, :], prob[:, 2:5, :]
        moeT = oT

        ps_turn = ps("ps_turn", [P, 2, S])
        ps_guard = ps("ps_guard", [P, 2, S])
        ps_score = ps("ps_score", [P, 2, S])
        ps_acc = ps("ps_acc", [P, 2, S])
        acc, mis = ps_acc[:, 0, :], ps_acc[:, 1, :]

        names = ("w_in x_in setup_pe setup_dve w_spilled w_turned dve_order xn_ready z_ready xnT_ps zT_ps xnT_ready "
                 "xfT_ready proj_ps proj_hi proj_done y_ready qk_spilled q_turned kq0 kq1 kq2 kq3 turn_ps rot_done "
                 "u_sum u_hi_done u_lo_done guard_ps max_done maxT_ps maxT_done row_out row_in score_ps exp_done pv_done "
                 "oT_done oTT_ps attn_done mg_ps mmax_done mmaxT_ps mmaxT_done mainrow_out mainrow_in main_done attnT_ps "
                 "attnT_ready wo_ps src2_ready z2T_ps x2T_ready logit_ps logit_ready esel_done gate_ready gateT_ps gateT_hi gateT_done "
                 "hid_ps relu_done gsel_ps hg_done moe_done moeT_ready moeTT_ps var_ready var_eps rstd_ready final_ready silu_in esig_done batch_done stored half_set x_free memset_done").split()
        s = {n: sem(n) for n in names}
        s_kq = [s[f"kq{i}"] for i in range(NQ)]
        per = dict(x_in=16, dve_order=None, xn_ready=1, z_ready=1, xnT_ps=1, zT_ps=1, xnT_ready=1, xfT_ready=1,
                   proj_ps=5, proj_hi=2, proj_done=3, y_ready=1, qk_spilled=64, q_turned=16 * 12, kq=64,
                   turn_ps=2 * H, rot_done=2 * H, u_sum=H, u_hi_done=H, u_lo_done=H, guard_ps=NT, max_done=NT,
                   maxT_ps=NQ, maxT_done=NQ, row_in=16 * NQ, row_out=16 * NQ, mainrow_out=16, score_ps=NT + T, exp_done=NT + T, pv_done=NQ * T + T,
                   oT_done=NQ, oTT_ps=NQ, attn_done=NQ, mg_ps=T, mmax_done=T + 1, mmaxT_ps=1, mmaxT_done=1,
                   mainrow_in=16, main_done=1, attnT_ps=1, attnT_ready=1, wo_ps=1, src2_ready=1, z2T_ps=1,
                   x2T_ready=1, logit_ps=1, logit_ready=1, esel_done=1, gate_ready=1, gateT_ps=1, gateT_hi=1, gateT_done=1,
                   hid_ps=E, relu_done=E, gsel_ps=E, hg_done=E, moe_done=E, moeT_ready=1, moeTT_ps=1,
                   final_ready=1, var_ready=3, var_eps=3, rstd_ready=3, silu_in=1, esig_done=1, batch_done=1, stored=16, x_free=1)
        NLINK = 22
        per["dve_order"] = NLINK
        NW = 30 * 16

        block = ctx.enter_context(nc.Block())

        def main_slot(jb):
            return jb

        def bank_of(n):
            return n % 2

        def pslot(n):
            return (n + T) % PSLOTS

        @block.sync
        def _(eng):
            def load(dst, src):
                eng.dma_start(dst, src).then_inc(s["w_in"], 16)

            eng.dma_start(xin[:, :, :], x[0].rearrange("(t p) d -> p t d", p=P)).then_inc(s["x_in"], 16)
            for dst, src in ((WqA, Wq), (WkA, Wk), (WvA, Wv)):
                load(dst[:, :, :], src.rearrange("(c p) d -> p c d", p=P))
            load(WoA, Wo)
            load(ident[:, :], c_ident)
            for n, src in enumerate((bq, bk, bv)):
                for c in range(2):
                    load(biasA[:, n, c:c + 1], src.rearrange("(c p o) -> c p o", c=2, o=1)[c])
            load(bo_row, bo.partition_broadcast(P))
            for dst, src in ((wqF, wq), (wkF, wk), (wvF, wv), (woF, wo), (selF, sel_w)):
                load(dst[:, :], src)
            for n, src in enumerate((ln1_g, ln1_b, ln2_g, ln2_b)):
                load(lnF[:, n:n + 1], src.rearrange("(p o) -> p o", o=1))
            load(wpF, wp)
            load(span, c_span)
            load(cosT[:, :], c_cos)
            load(sinT[:, :], c_sin)
            load(key_table, c_key)
            load(pick32[:, :], c_pick)
            load(iota[:, :, :], c_iota.rearrange("p (k e) -> p k e", k=TOPK))
            load(keysF[:, :, :], keys.rearrange("e d h -> d e h"))
            load(valsF[:, :, :], values.rearrange("e h d -> h e d"))

            eng.wait_ge(s["setup_dve"], 6)
            eng.dma_start(spill_w[0], w_hi[:, :].bitcast(F32)).then_inc(s["w_spilled"], 16)
            eng.dma_start(spill_w[1], w_lo[:, :].bitcast(F32)).then_inc(s["w_spilled"], 16)
            eng.wait_ge(s["w_spilled"], 32)
            for g in range(QH):
                for r, part in enumerate((0, 0, 1)):
                    src = spill_w[part].rearrange("(q g d) n -> g d q n", g=QH, d=HD)[g]
                    eng.dma_start(turn_w[32 * g + HD * r:32 * g + HD * (r + 1), :, :].bitcast(F32), src)\
                       .then_inc(s["w_turned"], 16)

            def batch(b):
                def wait(name, k):
                    eng.wait_ge(s[name], b * per[name] + k)

                def guard_row(q):
                    wait("maxT_done", q + 1)
                    eng.dma_start(spill_row[q], rowmaxT[:, q % 2, :].bitcast(F32)).then_inc(s["row_out"], 16)
                    wait("row_out", 16 * (q + 1))
                    eng.dma_start(u_hi[RQ:RK, q % USLOTS, :, :].bitcast(F32),
                                  spill_row[q].rearrange("(o g t) i -> o g (t i)", o=1, g=QH)).then_inc(s["row_in"], 16)

                wait("proj_done", 2)
                for n, src in enumerate((q_hi, q_lo, k_hi, k_lo)):
                    eng.dma_start(spill[n], src.bitcast(F32)).then_inc(s["qk_spilled"], 16)
                wait("qk_spilled", 64)
                for g in range(QH):
                    for r, part in enumerate((0, 1, 0)):
                        src = spill[part].rearrange("(q g d) i -> g d q i", g=QH, d=HD)[g]
                        eng.dma_start(turn_q[32 * g + HD * r:32 * g + HD * (r + 1), :, :].bitcast(F32), src)\
                           .then_inc(s["q_turned"], 16)
                for q in range(NQ):
                    if q == 1:
                        wait("mmaxT_done", 1)
                        eng.dma_start(spill_main, mainrowT[:, :]).then_inc(s["mainrow_out"], 16)
                        wait("mainrow_out", 16)
                        eng.dma_start(mainrow[:, :], spill_main.rearrange("(o t) i -> o (t i)", o=1))\
                           .then_inc(s["mainrow_in"], 16)
                    if q == USLOTS:
                        guard_row(0)
                        guard_row(1)
                        wait("score_ps", T + 16 * (q - USLOTS + 1))
                    for dst, part in ((u_hi, 0), (u_lo, 1), (k_hi4, 2), (k_lo4, 3)):
                        src = spill[part].rearrange("(q g d) i -> q d g i", g=QH, d=HD)[q]
                        eng.dma_start(dst[RF:RQ, q % USLOTS, :, :].bitcast(F32), src).then_inc(s_kq[q], 16)
                guard_row(2)
                guard_row(3)

            def load_x(b):
                eng.dma_start(xin[:, :, :], x[b].rearrange("(t p) d -> p t d", p=P)).then_inc(s["x_in"], 16)

            def store(b):
                eng.wait_ge(s["batch_done"], b + 2)
                eng.dma_start(out[b].rearrange("(t p) d -> p t d", p=P), zn[:, :, :]).then_inc(s["stored"], 16)

            with eng.Fori(0, B - 1) as b:
                batch(b)
                eng.wait_ge(s["x_free"], b + 1)
                load_x(b + 1)
                store(b)
            batch(B - 1)
            store(B - 1)
            eng.wait_ge(s["stored"], 16 * (B + 1))

        @block.tensor
        def _(eng):
            mm, tr = eng.matmul, eng.transpose
            eng.wait_ge(s["w_in"], NW)
            for c in range(2):
                tr(ps_turn[:, 0, c * P:(c + 1) * P], WoA[:, c * P:(c + 1) * P], ident[:, :])
            tail = mm(ps_turn[:, 1, 0:2 * RF], wpF, span, start=True, stop=True)
            tail.then_inc(s["setup_pe"], 1)
            eng.wait_ge(s["setup_dve"], 1)
            for c in range(2):
                mm(ps_score[:, 0, 0:P], WqA[:, c, :], WkA[:, c, :], start=c == 0, stop=c == 1)
            for c in range(2):
                mm(ps_score[:, 1, 0:P], WvA[:, c, :], WoT[:, c, :], start=c == 0, stop=c == 1)
            for c in range(2):
                mm(ps_guard[:, 0, 0:1], WkA[:, c, :], biasA[:, 0, c:c + 1], start=c == 0, stop=c == 1)
            for c in range(2):
                mm(ps_guard[:, 1, 0:1], WqA[:, c, :], biasA[:, 1, c:c + 1], start=c == 0, stop=c == 1)
            for c in range(2):
                mm(mis[:, 0:1], biasA[:, 0, c:c + 1].to_broadcast([P, P]), biasA[:, 1, c:c + 1],
                   start=c == 0, stop=c == 1)
            for c in range(2):
                tail = mm(acc[:, 0:P], biasA[:, 2, c:c + 1].to_broadcast([P, P]), WoT[:, c, :],
                          start=c == 0, stop=c == 1)
            tail.then_inc(s["setup_pe"], 1)
            eng.wait_ge(s["setup_dve"], 12)
            eng.wait_ge(s["w_turned"], 12 * 16)

            with eng.Fori(0, B) as b:
                def wait(name, k):
                    eng.wait_ge(s[name], b * per[name] + k)

                wait("xn_ready", 1)
                wait("batch_done", 1)
                for t in range(T):
                    tail = tr(mis[:, t * P:(t + 1) * P], xn[:, t, :], ident[:, :])
                tail.then_inc(s["xnT_ps"], 1)
                wait("z_ready", 1)
                for t in range(T):
                    tail = tr(ps_turn[:, 0, t * P:(t + 1) * P], zn[:, t, :], ident[:, :])
                tail.then_inc(s["zT_ps"], 1)
                wait("xfT_ready", 1)
                mm(ps_score[:, 0, :], wqF[:, :], xfT[:, :], start=True, stop=True).then_inc(s["proj_ps"], 1)
                mm(ps_score[:, 1, :], wkF[:, :], xfT[:, :], start=True, stop=True).then_inc(s["proj_ps"], 1)
                wait("xnT_ready", 1)
                mm(ps_turn[:, 1, :], wqk[:, :], xnT[:, :], start=True, stop=True).then_inc(s["proj_ps"], 1)
                for t in range(T):
                    tail = mm(ps_guard[:, t // 2, (t % 2) * (P + 1):(t % 2 + 1) * (P + 1)],
                              xnT[:, t * P:(t + 1) * P], wvo[:, :], start=t % 2 == 0, stop=t % 2 == 1,
                              skip_group_check=True)
                tail.then_inc(s["proj_ps"], 1)
                for t in range(T):
                    tail = mm(acc[:, t * P:(t + 1) * P], xfT[:, t * P:(t + 1) * P], wvF[:, :],
                              start=t == 0, stop=t == T - 1, skip_group_check=True)
                tail.then_inc(s["proj_ps"], 1)

                for tick in range(TICKS):
                    m = tick - MAIN_GUARD
                    if 0 <= m < T:
                        if m == 0:
                            wait("y_ready", 1)
                            wait("proj_done", 3)
                        if m >= 2:
                            wait("mmax_done", m - 1)
                        mm(ps_score[:, m % 2, :], yT[:, m * P:(m + 1) * P], xnT[:, :],
                           start=True, stop=True).then_inc(s["mg_ps"], 1)
                    if tick == MAIN_ROW:
                        wait("mmax_done", T + 1)
                        tr(mis[0:T, 0:P], mmax[:, 2, :], ident[:, :]).then_inc(s["mmaxT_ps"], 1)
                    m = (tick - MAIN_SCORE)
                    if 0 <= m < 2 * T and m % 2 == 0:
                        jb = m // 2
                        if jb == 0:
                            wait("mainrow_in", 16)
                        if jb >= 2:
                            wait("exp_done", jb - 1)
                        mm(ps_score[:, jb % 2, :], xnT[:, jb * P:(jb + 1) * P], yT[:, :], start=True, stop=False)
                        mm(ps_score[:, jb % 2, :], ones_row[:, :], mainrow[:, :], start=False, stop=True)\
                            .then_inc(s["score_ps"], 1)
                    if 2 <= m < 2 * T + 2 and m % 2 == 0:
                        jb = m // 2 - 1
                        wait("exp_done", jb + 1)
                        for ib in range(T):
                            tail = mm(ps_acc[:, ib // 2, (ib % 2) * (P + 1):(ib % 2 + 1) * (P + 1)],
                                      prob[:, main_slot(jb), ib * P:(ib + 1) * P], vmain[:, jb, :],
                                      start=jb == 0 and ib % 2 == 0, stop=jb == T - 1 and ib % 2 == 1,
                                      skip_group_check=True)
                        tail.then_inc(s["pv_done"], 1)

                    if tick % 4 == 0 and tick // 4 < H:
                        h = tick // 4
                        g = h % QH
                        if h == 0:
                            wait("q_turned", 12 * 16)
                        if h >= 1:
                            wait("rot_done", 2 * h - 1)
                        rows = slice(32 * g, 32 * g + 3 * HD)
                        mm(ps_turn[0:RF, 0, :], turn_w[rows, h // QH, 0:RF], turn_q[rows, h // QH, :],
                           start=True, stop=True).then_inc(s["turn_ps"], 1)
                        if h >= 1:
                            wait("rot_done", 2 * h)
                        mm(ps_turn[0:RF, 1, :], turn_w[rows, h // QH, RF:2 * RF], turn_q[rows, h // QH, :],
                           start=True, stop=True).then_inc(s["turn_ps"], 1)
                    n = tick - SCORE_AT
                    if 0 <= n < NT:
                        q, jb, g = n // 16, n // 4 % 4, n % 4
                        slot = q % USLOTS
                        if n % 16 == 0:
                            wait("u_lo_done", QH * (q + 1))
                            wait("row_in", 16 * (q + 1))
                        wait("exp_done", T + n - 1)
                        ko = slice(jb * P, (jb + 1) * P)
                        o = ps_score[:, bank_of(n), :]
                        mm(o, k_hi4[0:RK, slot, g, ko], u_hi[0:RK, slot, g, :], start=True, stop=False)
                        mm(o, k_hi4[0:RK, slot, g, ko], u_lo[0:RK, slot, g, :], start=False, stop=False)
                        mm(o, k_lo4[0:RK, slot, g, ko], u_hi[0:RK, slot, g, :], start=False, stop=True)\
                            .then_inc(s["score_ps"], 1)
                    n = tick - GUARD_AT
                    if 0 <= n < NT:
                        h, ib = n // T, n % T
                        q, g = h // QH, h % QH
                        if ib == 0:
                            wait("u_hi_done", h + 1)
                        if n % 16 == 0:
                            eng.wait_ge(s_kq[q], b * per["kq"] + 64)
                        if n >= 2:
                            wait("max_done", n - 1)
                        mm(ps_guard[:, n % 2, :], u_hi[0:RQ, q % USLOTS, g, ib * P:(ib + 1) * P],
                           k_hi4[0:RQ, q % USLOTS, g, :], start=True, stop=True).then_inc(s["guard_ps"], 1)
                    n = tick - GUARD_AT - 16
                    if n >= 0 and n % 16 == 0 and n // 16 < NQ:
                        q = n // 16
                        wait("max_done", 16 * (q + 1))
                        if q == 0:
                            wait("main_done", 1)
                        else:
                            wait("maxT_done", q)
                        if q >= 2:
                            wait("attn_done", q - 1)
                        tr(mis[0:QH * T, 0:P], rowmax[:, q % 2, :], ident[:, :]).then_inc(s["maxT_ps"], 1)
                    n = tick - SCORE_AT - 6
                    if n >= 0 and n % 4 == 0 and n // 4 < NQ * T:
                        m = n // 4
                        q, jb = m // T, m % T
                        wait("exp_done", T + 4 * (m + 1))
                        if jb == 0:
                            if q == 0:
                                wait("main_done", 1)
                            else:
                                wait("oT_done", q)
                        for g in range(QH):
                            c = (QH * q + g) * (HD + 1)
                            tail = mm(acc[32 * g:32 * g + 32, :], vhead[:, jb, c:c + 32],
                                      prob[:, pslot(4 * m + g), :], start=jb == 0, stop=jb == T - 1)
                        tail.then_inc(s["pv_done"], 1)
                    n = tick - SCORE_AT - 21
                    if n >= 0 and n % 16 == 0 and n // 16 < NQ:
                        q = n // 16
                        wait("oT_done", q + 1)
                        wait("maxT_done", min(q + 2, NQ))
                        if q >= 1:
                            wait("attn_done", q)
                        for t in range(T):
                            tail = tr(mis[:, t * P:(t + 1) * P], oT[:, t * P:(t + 1) * P], ident[:, :])
                        tail.then_inc(s["oTT_ps"], 1)

                wait("attn_done", NQ)
                for t in range(T):
                    tail = tr(mis[:, t * P:(t + 1) * P], attn[:, t, :, :].rearrange("p h d -> p (h d)"), ident[:, :])
                tail.then_inc(s["attnT_ps"], 1)
                wait("attnT_ready", 1)
                for t in range(T):
                    tail = mm(acc[:, t * P:(t + 1) * P], attnT[:, t * P:(t + 1) * P], woF[:, :],
                              start=t == 0, stop=t == T - 1, skip_group_check=True)
                tail.then_inc(s["wo_ps"], 1)
                wait("src2_ready", 1)
                for t in range(T):
                    tail = tr(mis[:, t * P:(t + 1) * P], zn[:, t, :], ident[:, :])
                tail.then_inc(s["z2T_ps"], 1)
                wait("x2T_ready", 1)
                for t in range(T):
                    tail = mm(acc[:, t * E:(t + 1) * E], x2T[:, t * P:(t + 1) * P], selF[:, :],
                              start=t == 0, stop=t == T - 1, skip_group_check=True)
                tail.then_inc(s["logit_ps"], 1)

                def hidden(e):
                    if e >= 2:
                        wait("relu_done", e - 1)
                    mm(ps_score[:, e % 2, :], keysF[:, e, :], x2T[:, :], start=True, stop=True)\
                        .then_inc(s["hid_ps"], 1)

                hidden(0)
                hidden(1)
                wait("gate_ready", 1)
                for t in range(T):
                    tail = tr(mis[0:E, t * P:(t + 1) * P], gate[:, t, :], ident[:, :])
                tail.then_inc(s["gateT_ps"], 1)
                wait("gateT_done", 1)
                for e in range(E + 2):
                    if e < E:
                        if e >= 2:
                            hidden(e)
                            wait("hg_done", e - 1)
                        mm(ps_guard[:, e % 2, :], pick[:, e:e + 1].to_broadcast([2 * E, P]), gateT[:, :],
                           start=True, stop=True).then_inc(s["gsel_ps"], 1)
                    if e >= 2:
                        f = e - 2
                        wait("hg_done", f + 1)
                        if f == 0:
                            wait("esel_done", 1)
                        mm(acc, valsF[:, f, :], hgate[:, f % 3, :], start=f == 0, stop=f == E - 1)\
                            .then_inc(s["moe_done"], 1)
                wait("moeT_ready", 1)
                for t in range(T):
                    tail = tr(mis[:, t * P:(t + 1) * P], moeT[:, t * P:(t + 1) * P], ident[:, :])
                tail.then_inc(s["moeTT_ps"], 1)

        @block.vector
        def _(eng):
            V = eng

            def setup(ins):
                ins.then_inc(s["setup_dve"], 1)

            V.memset(k_hi4[96:P, :, :, :].bitcast(F32), 1.0).then_inc(s["memset_done"], 1)
            V.memset(k_lo4[96:P, :, :, :].bitcast(F32), 0.0).then_inc(s["memset_done"], 1)
            V.memset(u_lo[96:P, :, :, :].bitcast(F32), 0.0).then_inc(s["memset_done"], 1)
            V.memset(vhead[:, :, :], 1.0).then_inc(s["memset_done"], 1)
            V.memset(vmain[:, :, :], 1.0).then_inc(s["memset_done"], 1)
            V.memset(ones_row[:, :], 1.0).then_inc(s["memset_done"], 1)
            V.wait_ge(s["memset_done"], 6)
            V.wait_ge(s["w_in"], NW)
            V.wait_ge(s["setup_pe"], 1)
            setup(V.tensor_copy(WoT[:, :, :], ps_turn[:, 0, 0:2 * P].rearrange("p (c n) -> p c n", c=2)))
            setup(V.tensor_copy(w_hi[:, :], ps_turn[:, 1, 0:2 * RF]))
            setup(V.tensor_copy(k_hi4[0:RF, 0, 0, :], key_table))
            setup(V.tensor_copy(pick[:, :], pick32[:, :]))
            V.wait_ge(s["setup_dve"], 4)
            setup(V.tensor_tensor(w_lo[:, :], ps_turn[:, 1, 0:2 * RF], w_hi[:, :].bitcast(F32), ALU.subtract))
            setup(V.tensor_tensor(k_lo4[0:RF, 0, 0, :], key_table, k_hi4[0:RF, 0, 0, :].bitcast(F32),
                                  ALU.subtract))
            V.wait_ge(s["setup_dve"], 6)
            for i in range(1, USLOTS * QH):
                V.tensor_copy(k_hi4[0:RF, i // QH, i % QH, :], k_hi4[0:RF, 0, 0, :].bitcast(F32))
                V.tensor_copy(k_lo4[0:RF, i // QH, i % QH, :], k_lo4[0:RF, 0, 0, :].bitcast(F32))
            V.wait_ge(s["setup_pe"], 2)
            setup(V.tensor_copy(wqk[:, :], ps_score[:, 0, 0:P]))
            setup(V.tensor_copy(wvo[:, 0:P], ps_score[:, 1, 0:P]))
            setup(V.tensor_copy(y_bias[:, :], ps_guard[:, 0, 0:1]))
            setup(V.tensor_copy(wvo[:, P:P + 1], ps_guard[:, 1, 0:1]))
            setup(V.tensor_copy(bqbk[:, :], mis[:, 0:1]))
            setup(V.tensor_tensor(out_bias[:, :], acc[:, 0:P], bo_row, ALU.add))
            V.wait_ge(s["setup_dve"], 12)
            V.memset(carrier[:, :], 0.0).then_inc(s["batch_done"], 1)
            V.memset(rhead[:, :, :], 0.0).then_inc(s["stored"], 16)

            with eng.Fori(0, B) as b:
                def wait(name, k):
                    eng.wait_ge(s[name], b * per[name] + k)

                links = [0]
                norms = [0]

                def link(ins, fixed=False):
                    links[0] += 1
                    ins.then_inc(s["dve_order"], 1)
                    wait("dve_order", links[0])
                    if fixed:
                        V.memset(carrier[:, :], 0.0)

                def normalise(dst, src, done):
                    for t in range(T):
                        i = V.bn_stats(stats[:, t, :], src[:, t, :])
                    link(i, fixed=True)
                    for t in range(T):
                        i = V.bn_aggr(mv[:, t, :], stats[:, t, :])
                    i.then_inc(s["var_ready"], 1)
                    norms[0] += 1
                    wait("rstd_ready", norms[0])
                    for t in range(T):
                        i = V.tensor_scalar(dst[:, t, :], src[:, t, :], mv[:, t, 0:1], rstd[:, t:t + 1],
                                            ALU.subtract, ALU.mult)
                    i.then_inc(s[done], 1)

                wait("x_in", 16)
                wait("batch_done", 1)
                normalise(xn, xin, "xn_ready")
                wait("xn_ready", 1)
                wait("stored", 16)
                normalise(zn, xn, "z_ready")
                V.tensor_copy(xres[:, :, :], xin[:, :, :]).then_inc(s["x_free"], 1)
                wait("zT_ps", 1)
                V.tensor_scalar(xfT[:, :], ps_turn[:, 0, :], lnF[:, 0:1], lnF[:, 1:2], ALU.mult, ALU.add)\
                    .then_inc(s["xfT_ready"], 1)
                for n, (lo, hi) in enumerate(((q_lo, q_hi), (k_lo, k_hi))):
                    wait("proj_hi", n + 1)
                    V.tensor_tensor(lo, ps_score[:, n, :], hi.bitcast(F32), ALU.subtract)\
                        .then_inc(s["proj_done"], 1)
                wait("proj_ps", 4)
                for c in range(2):
                    pv = ps_guard[:, c, 0:2 * (P + 1)].rearrange("p (t n) -> p t n", t=2)
                    V.tensor_copy(vmain[:, 2 * c:2 * c + 2, 0:P], pv[:, :, 0:P])
                    i = V.tensor_scalar(cmain[:, 2 * c:2 * c + 2], pv[:, :, P], bqbk[:, 0:1], None, ALU.add)
                link(i)
                wait("proj_ps", 5)
                V.tensor_copy(vhead[:, :, 0:H * (HD + 1)].rearrange("p t (h c) -> p t h c", h=H)[:, :, :, 0:HD],
                              acc.rearrange("p (t h c) -> p t h c", t=T, h=H)).then_inc(s["proj_done"], 1)

                for tick in range(TICKS):
                    m = tick - MAIN_GUARD
                    if 0 <= m < T:
                        wait("mg_ps", m + 1)
                        V.tensor_reduce(mmax[:, 0, m:m + 1], ps_score[:, m % 2, :], X, ALU.max)\
                            .then_inc(s["mmax_done"], 1)
                    if tick == T - 1:
                        wait("mmax_done", T)
                        link(V.tensor_tensor(mmax[:, 1, :], mmax[:, 0, :], cmain[:, :], ALU.add))
                        V.tensor_tensor(mmax[:, 2, :], cmain[:, :], mmax[:, 1, :], ALU.subtract)\
                            .then_inc(s["mmax_done"], 1)
                    if tick == MAIN_OUT:
                        wait("pv_done", T)
                        for c in range(2):
                            pa = ps_acc[:, c, 0:2 * (P + 1)].rearrange("p (t n) -> p t n", t=2)
                            i = V.reciprocal(rmain[:, 2 * c:2 * c + 2], pa[:, :, P])
                        link(i)
                        for t in range(T):
                            o = (t % 2) * (P + 1)
                            i = V.scalar_tensor_tensor(smain[:, t, :], ps_acc[:, t // 2, o:o + P], rmain[:, t:t + 1],
                                                       out_bias[:, :], ALU.mult, ALU.add)
                        i.then_inc(s["main_done"], 1)
                    n = tick - GUARD_AT
                    if 0 <= n < NT:
                        q = n // 16
                        if n % 16 == 0 and q >= 2:
                            wait("maxT_ps", q - 1)
                        wait("guard_ps", n + 1)
                        V.tensor_reduce(rowmax[:, q % 2, n % 16:n % 16 + 1], ps_guard[:, n % 2, :], X, ALU.max)\
                            .then_inc(s["max_done"], 1)
                    if tick % 4 == 0 and tick // 4 < H:
                        h = tick // 4
                        if h >= 2:
                            wait("u_lo_done", h - 1)
                        wait("turn_ps", 2 * h + 1)
                        V.tensor_tensor(rot_a[:, h % 2, :], ps_turn[0:RF, 0, :], cosT[:, :], ALU.mult)\
                            .then_inc(s["rot_done"], 1)
                        wait("turn_ps", 2 * h + 2)
                        V.tensor_tensor(rot_b[:, h % 2, :], ps_turn[0:RF, 1, :], sinT[:, :], ALU.mult)\
                            .then_inc(s["rot_done"], 1)
                    n = tick - SCORE_AT - 22
                    if n >= 0 and n % 16 == 0 and n // 16 < NQ:
                        q = n // 16
                        wait("oTT_ps", q + 1)
                        pt = mis.rearrange("p (t g r) -> p t g r", t=T, g=QH)
                        link(V.reciprocal(rhead[:, :, :], pt[:, :, :, HD]))
                        V.tensor_tensor(attn[:, :, QH * q:QH * q + QH, :], pt[:, :, :, 0:HD],
                                        rhead[:, :, :].unsqueeze(3).to_broadcast([P, T, QH, HD]), ALU.mult)\
                            .then_inc(s["attn_done"], 1)

                wait("wo_ps", 1)
                link(V.tensor_tensor(src2[:, :, :], acc.rearrange("p (t d) -> p t d", t=T), xn[:, :, :], ALU.add))
                normalise(zn, src2, "src2_ready")
                wait("z2T_ps", 1)
                V.tensor_scalar(x2T[:, :], mis, lnF[:, 2:3], lnF[:, 3:4], ALU.mult, ALU.add)\
                    .then_inc(s["x2T_ready"], 1)
                wait("logit_ps", 1)
                V.tensor_scalar(selx[:, :, :], acc[:, 0:T * E].rearrange("p (t e) -> p t e", t=T), -87.0, None,
                                ALU.max).then_inc(s["logit_ready"], 1)
                wait("esel_done", 1)
                link(V.tensor_scalar(selx[:, :, :], sel[:, :, :], 1.0, None, ALU.add))
                link(V.reciprocal(sel[:, :, :], selx[:, :, :]), fixed=True)
                for t in range(T):
                    i = V.max(top[:, t, :], sel[:, t, :])
                link(i, fixed=True)
                for t in range(T):
                    i = V.max_index(topi[:, t, :], top[:, t, :], sel[:, t, :])
                link(i)
                link(V.tensor_copy(topf[:, :, :], topi[:, :, :]))
                for t in range(T):
                    i = V.tensor_tensor(hit[:, t, :, :], iota[:, :, :],
                                        topf[:, t, 0:TOPK].unsqueeze(2).to_broadcast([P, TOPK, E]), ALU.is_equal)
                link(i)
                link(V.tensor_reduce(selx[:, :, :], hit[:, :, :, :].rearrange("p t k e -> p t e k"), X, ALU.add))
                V.tensor_tensor(gate[:, :, :], sel[:, :, :], selx[:, :, :], ALU.mult).then_inc(s["gate_ready"], 1)
                wait("gateT_hi", 1)
                V.tensor_tensor(gateT[E:2 * E, :], mis[0:E, :], gateT[0:E, :].bitcast(F32), ALU.subtract)\
                    .then_inc(s["gateT_done"], 1)

                for e in range(E):
                    wait("relu_done", e + 1)
                    wait("gsel_ps", e + 1)
                    if e >= 3:
                        wait("moe_done", e - 2)
                    V.tensor_tensor(hgate[:, e % 3, :], ps_guard[:, e % 2, :], hrelu[:, e % 2, :], ALU.mult)\
                        .then_inc(s["hg_done"], 1)

                wait("moeTT_ps", 1)
                V.tensor_tensor(xn[:, :, :], mis.rearrange("p (t d) -> p t d", t=T), src2[:, :, :], ALU.add)\
                    .then_inc(s["final_ready"], 1)
                wait("final_ready", 1)
                V.tensor_scalar(attn[:, :, :, :].rearrange("p t h d -> p t (h d)"), xn[:, :, :], -87.0, None, ALU.max)\
                    .then_inc(s["silu_in"], 1)
                link(V.tensor_tensor(src2[:, :, :], xn[:, :, :], smain[:, :, :], ALU.mult))
                wait("esig_done", 1)
                link(V.tensor_scalar(smain[:, :, :], zn[:, :, :], 1.0, None, ALU.add))
                link(V.reciprocal(xn[:, :, :], smain[:, :, :]))
                link(V.tensor_tensor(smain[:, :, :], src2[:, :, :], xn[:, :, :], ALU.mult))
                V.tensor_tensor(zn[:, :, :], smain[:, :, :], xres[:, :, :], ALU.add).then_inc(s["batch_done"], 1)

                assert links[0] == NLINK, links[0]

        @block.scalar
        def _(eng):
            with eng.Fori(0, B) as b:
                def wait(name, k):
                    eng.wait_ge(s[name], b * per[name] + k)

                wait("xnT_ps", 1)
                eng.activation(xnT[:, :], mis, ACT.Copy).then_inc(s["xnT_ready"], 1)
                for n, hi in enumerate((q_hi, k_hi)):
                    wait("proj_ps", n + 1)
                    eng.activation(hi, ps_score[:, n, :], ACT.Copy).then_inc(s["proj_hi"], 1)
                wait("proj_ps", 3)
                eng.activation(yT[:, :], ps_turn[:, 1, :], ACT.Identity, bias=y_bias[:, 0:1]).then_inc(s["y_ready"], 1)

                for tick in range(TICKS):
                    if tick == MAIN_ROW:
                        wait("mmaxT_ps", 1)
                        eng.activation(mainrowT[:, :], mis[0:T, 0:P], ACT.Copy).then_inc(s["mmaxT_done"], 1)
                    m = tick - MAIN_SCORE
                    if 0 <= m < 2 * T and m % 2 == 0:
                        jb = m // 2
                        wait("score_ps", jb + 1)
                        eng.activation(prob[:, main_slot(jb), :], ps_score[:, jb % 2, :], ACT.Exp, scale=MAIN_SCALE)\
                            .then_inc(s["exp_done"], 1)
                    n = tick - SCORE_AT
                    if 0 <= n < NT:
                        m = n // 4
                        wait("score_ps", T + n + 1)
                        if n % 4 == 0:
                            wait("pv_done", T if m < 2 else T + m - 1)
                        eng.activation(prob[:, pslot(n), :], ps_score[:, bank_of(n), :], ACT.Exp, scale=HEAD_SCALE)\
                            .then_inc(s["exp_done"], 1)
                    if tick % 4 == 2 and tick // 4 < H:
                        h = tick // 4
                        q = h // QH
                        wait("u_sum", h + 1)
                        if q >= USLOTS:
                            wait("score_ps", T + 16 * (q - USLOTS + 1))
                        eng.activation(u_hi[0:RF, q % USLOTS, h % QH, :], rot_a[:, h % 2, :], ACT.Copy)\
                            .then_inc(s["u_hi_done"], 1)
                    n = tick - GUARD_AT - 16
                    if n >= 0 and n % 16 == 0 and n // 16 < NQ:
                        q = n // 16
                        wait("maxT_ps", q + 1)
                        if q >= 2:
                            wait("row_in", 16 * (q - 1))
                        eng.activation(rowmaxT[:, q % 2, :], mis[0:QH * T, 0:P], ACT.Copy, scale=-1.0)\
                            .then_inc(s["maxT_done"], 1)
                    n = tick - SCORE_AT - 20
                    if n >= 0 and n % 16 == 0 and n // 16 < NQ:
                        q = n // 16
                        wait("pv_done", T + T * (q + 1))
                        if q >= 1:
                            wait("oTT_ps", q)
                        eng.activation(oT[:, :], acc, ACT.Copy).then_inc(s["oT_done"], 1)

                wait("attnT_ps", 1)
                eng.activation(attnT[:, :], mis, ACT.Copy).then_inc(s["attnT_ready"], 1)
                wait("logit_ready", 1)
                eng.activation(sel[:, :, :], selx[:, :, :], ACT.Exp, scale=-1.0)\
                    .then_inc(s["esel_done"], 1)
                for e in range(E):
                    if e == 2:
                        wait("gateT_ps", 1)
                        eng.activation(gateT[0:E, :], mis[0:E, :], ACT.Copy).then_inc(s["gateT_hi"], 1)
                    wait("hid_ps", e + 1)
                    if e >= 2:
                        wait("hg_done", e - 1)
                    eng.activation(hrelu[:, e % 2, :], ps_score[:, e % 2, :], ACT.Relu).then_inc(s["relu_done"], 1)
                wait("moe_done", E)
                eng.activation(moeT[:, :], acc, ACT.Copy).then_inc(s["moeT_ready"], 1)
                wait("silu_in", 1)
                eng.activation(zn[:, :, :], attn[:, :, :, :].rearrange("p t h d -> p t (h d)"), ACT.Exp, scale=-1.0).then_inc(s["esig_done"], 1)

        @block.gpsimd
        def _(eng):
            eng.memset(minus_half[:, :], -0.5).then_inc(s["half_set"], 1)
            eng.memset(eps[:, :], EPS).then_inc(s["half_set"], 1)
            eng.wait_ge(s["half_set"], 2)
            with eng.Fori(0, B) as b:
                def wait(name, k):
                    eng.wait_ge(s[name], b * per[name] + k)

                def add(h):
                    wait("rot_done", 2 * h + 2)
                    eng.tensor_tensor(rot_a[:, h % 2, :], rot_a[:, h % 2, :], rot_b[:, h % 2, :], ALU.add)\
                       .then_inc(s["u_sum"], 1)

                def low(h):
                    q = h // QH
                    wait("u_hi_done", h + 1)
                    if q >= USLOTS:
                        wait("score_ps", T + 16 * (q - USLOTS + 1))
                    eng.tensor_tensor(u_lo[0:RF, q % USLOTS, h % QH, :], rot_a[:, h % 2, :],
                                      u_hi[0:RF, q % USLOTS, h % QH, :].bitcast(F32), ALU.subtract)\
                       .then_inc(s["u_lo_done"], 1)

                def root(n):
                    wait("var_ready", n + 1)
                    eng.tensor_tensor(var_eps[:, :], mv[:, :, 1], eps[:, :], ALU.add).then_inc(s["var_eps"], 1)
                    wait("var_eps", n + 1)
                    eng.tensor_tensor(rstd[:, :], var_eps[:, :], minus_half[:, :], ALU.pow)\
                       .then_inc(s["rstd_ready"], 1)

                root(0)
                root(1)
                add(0)
                for h in range(H):
                    if h + 1 < H:
                        add(h + 1)
                    low(h)
                root(2)


_INS = ['L0_attn_hidden_states', 'L0_attn_Wq', 'L0_attn_bq', 'L0_attn_Wk', 'L0_attn_bk', 'L0_attn_Wv', 'L0_attn_bv',
        'L0_attn_Wo', 'L0_attn_bo', 'L0_ffn_wq', 'L0_ffn_wk', 'L0_ffn_wv', 'L0_ffn_wp', 'L0_ffn_wo', 'L0_ffn_ln1_g',
        'L0_ffn_ln1_b', 'L0_ffn_ln2_g', 'L0_ffn_ln2_b', 'L0_ffn_sel_w', 'L0_ffn_keys', 'L0_ffn_values']
_CONSTS = ["c_span", "c_cos", "c_sin", "c_key", "c_ident", "c_pick", "c_iota"]


def kernel(**inputs):
    import numpy as _np
    import concourse.bacc as _bacc
    from concourse import mybir as _mybir
    from concourse.bass_utils import run_bass_kernel_spmd as _run

    nc = _bacc.Bacc("TRN2", target_bir_lowering=False, num_devices=1)
    arrays, args = {}, []
    tables = position_constants()
    for name in _INS + _CONSTS:
        a = _np.ascontiguousarray(inputs[name] if name in inputs else tables[name])
        arrays[f"in_{name}_dram"] = a
        args.append(nc.dram_tensor(f"in_{name}_dram", a.shape, _mybir.dt.from_np(a.dtype), kind="ExternalInput").ap())
    args.append(nc.dram_tensor("out_0_dram", (B, S, P), F32, kind="ExternalOutput").ap())
    build(nc, *args)
    r = _run(nc, [arrays], core_ids=[0])
    return r.results[0]["out_0_dram"]
```

```python
from contextlib import ExitStack

import concourse.bass as bass
from concourse import mybir

F32 = mybir.dt.float32
FR = mybir.dt.float32r
U32 = mybir.dt.uint32
ALU = mybir.AluOpType
ACT = mybir.ActivationFunctionType
X = mybir.AxisListType.X

P = 128
B, S = 8, 512
T = S // P
H, HD = 16, 8
E, TOPK = 32, 4
NF = 59
RF = 2 * NF
RQ = RF + HD
RK = RQ + 1
QH = 4
NQ = H // QH
CE = S // P
NC = E // CE
USLOTS = 3
PSLOTS = 8
EPS = 1e-5
HEAD_SCALE = float(HD) ** -0.5
MAIN_SCALE = float(P) ** -0.5

GUARD_AT = 6
SCORE_AT = 27
NT = H * T
TICKS = SCORE_AT + NT + 10
MAIN_GUARD, MAIN_ROW, MAIN_SCORE, MAIN_OUT = 0, 4, 11, 20

V_STATS1, V_MEAN1, V_NORM1, V_STATS2, V_MEAN2, V_NORM2 = 2, 3, 4, 5, 6, 7
LAG = 3
PE_XN, ACT_XN, PE_Z, V_Z = 6, 7, 9, 10
PE_QK, ACT_QK, V_QK = 12, 13, 14
PE_Y, ACT_Y, V_VM0, PE_V, V_VM1, V_VHEAD = 16, 17, 17, 19, 20, 21


def position_constants():
    import numpy as np

    freq = 1.0 / 10000.0 ** (np.arange(0, P, 2) / P)
    keep = 44
    n = NF - keep
    nodes2 = freq[keep] ** 2 * (1 + np.cos((2 * np.arange(n) + 1) * np.pi / (2 * n))) / 2
    nodes = np.sqrt(nodes2)
    low = freq[keep:]
    lag = np.array([[np.prod([(f * f - nodes2[m]) / (nodes2[k] - nodes2[m]) for m in range(n) if m != k])
                     for f in low] for k in range(n)])
    span = np.zeros((P, 2 * NF))
    for k in range(keep):
        span[k, k] = span[P // 2 + k, NF + k] = 1.0
    span[keep:P // 2, keep:NF] = (lag * low[None, :] / nodes[:, None]).T
    span[P // 2 + keep:, NF + keep:] = lag.T
    f = np.concatenate([freq[:keep], nodes])
    at = f[:, None] * np.arange(S)[None, :]
    sin, cos = np.sin(at), np.cos(at)
    swapped = np.concatenate([span[:, NF:], span[:, :NF]], axis=1)
    f32 = np.float32
    return {
        "c_span": np.concatenate([span, swapped], axis=1).astype(f32),
        "c_cos": np.concatenate([cos, cos]).astype(f32),
        "c_sin": np.concatenate([sin, -sin]).astype(f32),
        "c_key": np.concatenate([sin, cos]).astype(f32),
        "c_ident": np.eye(P, dtype=f32),
        "c_pick": np.concatenate([np.eye(E), np.eye(E)]).astype(f32),
        "c_iota": np.tile(np.arange(E, dtype=f32), (P, TOPK)),
    }


def build(nc, x, Wq, bq, Wk, bk, Wv, bv, Wo, bo, wq, wk, wv, wp, wo, ln1_g, ln1_b, ln2_g, ln2_b,
          sel_w, keys, values, c_span, c_cos, c_sin, c_key, c_ident, c_pick, c_iota, out):
    spill = nc.dram_tensor("spill", (4, P, S), F32, kind="Internal").ap()
    spill_w = nc.dram_tensor("spill_w", (2, P, 2 * RF), F32, kind="Internal").ap()
    low_keys = nc.dram_tensor("low_keys", (P, NC, S), F32, kind="Internal").ap()
    low_vals = nc.dram_tensor("low_vals", (P, NC, S), F32, kind="Internal").ap()
    spill_row = nc.dram_tensor("spill_row", (NQ, QH * T, P), F32, kind="Internal").ap()
    spill_main = nc.dram_tensor("spill_main", (T, P), F32, kind="Internal").ap()

    with ExitStack() as ctx:
        def sb(name, shape, dt=F32):
            return ctx.enter_context(nc.sbuf_tensor(name, shape, dt))

        def ps(name, shape, dt=F32):
            return ctx.enter_context(nc.psum_tensor(name, shape, dt))

        def sem(name):
            return ctx.enter_context(nc.semaphore(name))

        ident = sb("ident", [P, P])
        rot_a = sb("rot_a", [P, 2, S])
        rot_b = sb("rot_b", [P, 2, S])
        xres = sb("xres", [P, T, P])
        key_table = xres[0:RF, :, :].rearrange("p t d -> p (t d)")
        halves = [(rot_a, rot_b)[n // 4][:, n // 2 % 2, (n % 2) * 2 * P:(n % 2 + 1) * 2 * P] for n in range(6)]
        WqA, WkA, WvA, WoT = (v.rearrange("p (c n) -> p c n", c=2) for v in halves[0:4])
        WoA, span = halves[4], halves[5][:, 0:2 * RF]
        wpF, bo_row = rot_b[:, 1, 0:P], rot_b[:, 1, P:2 * P]
        prob = sb("prob", [P, PSLOTS, S])
        biasA = sb("biasA", [P, 3, 2])
        wqk = sb("wqk", [P, P])
        wvo = sb("wvo", [P, P + 1])
        y_bias = sb("y_bias", [P, 1])
        bqbk = sb("bqbk", [P, 1])
        out_bias = sb("out_bias", [P, P])
        wqF, wkF, wvF, woF = (sb(n, [P, P]) for n in ("wqF", "wkF", "wvF", "woF"))
        selF = sb("selF", [P, E])
        lnF = sb("lnF", [P, 4])
        keys_hi = sb("keys_hi", [P, E, P], FR)
        vals_hi = sb("vals_hi", [P, E, P], FR)
        cosT = sb("cosT", [RF, S])
        sinT = sb("sinT", [RF, S])
        pick = sb("pick", [2 * E, E], FR)
        iota = sb("iota", [P, TOPK, E])
        turn_w = sb("turn_w", [P, NQ, 2 * RF], FR)

        xin = sb("xin", [P, T, P])
        xn = sb("xn", [P, T, P])
        zn = sb("zn", [P, T, P])
        stats = sb("stats", [P, T, 6])
        mv = sb("mv", [P, T, 2])
        carrier = sb("carrier", [P, 1])
        rstd = sb("rstd", [P, T])
        var_eps = sb("var_eps", [P, T])
        eps = sb("eps", [P, T])
        minus_half = sb("minus_half", [P, T])
        xnT = sb("xnT", [P, S])
        xfT = sb("xfT", [P, S])
        yT = sb("yT", [P, S])
        vmain = sb("vmain", [P, T, P + 1])
        cmain = sb("cmain", [P, T])
        turn_q = sb("turn_q", [P, NQ, S], FR)
        vhead = sb("vhead", [P, T, H * (HD + 1) + 32])
        u_hi = sb("u_hi", [P, USLOTS, QH, S], FR)
        u_lo = sb("u_lo", [P, USLOTS, QH, S], FR)
        w_hi, w_lo = u_lo[:, 0, 0, 0:2 * RF], u_lo[:, 0, 1, 0:2 * RF]
        def keys_lo(e):
            c, o = e // CE, e % CE * P
            return u_lo[:, 1 + c // QH, c % QH, o:o + P]

        def vals_lo(e):
            return u_lo[:, 0, e // CE % QH, e % CE * P:(e % CE + 1) * P]

        vals_low_stage = u_hi[:, 0:2, :, :].rearrange("p u g i -> p (u g) i")
        keys_low_stage = u_lo[:, 1:3, :, :].rearrange("p u g i -> p (u g) i")

        q_hi, q_lo, k_hi, k_lo = (u_hi[:, USLOTS - 1, n, :] for n in range(4))
        k_hi4 = sb("k_hi4", [P, USLOTS, QH, S], FR)
        k_lo4 = sb("k_lo4", [P, USLOTS, QH, S], FR)
        rowmax = sb("rowmax", [P, 2, QH * T])
        rowmaxT = sb("rowmaxT", [QH * T, 2, P], FR)
        mmax = sb("mmax", [P, 3, T])
        mainrowT = sb("mainrowT", [T, P], FR)
        mainrow = u_hi[0:1, USLOTS - 1, 0, :]
        ones_row = sb("ones_row", [1, P], FR)
        smain = sb("smain", [P, T, P])
        rmain = sb("rmain", [P, T])
        oT = sb("oT", [P, S])
        rhead = sb("rhead", [P, T, QH])
        attn = sb("attn", [P, T, H, HD])
        attnT = oT
        src2 = sb("src2", [P, T, P])
        res = sb("res", [P, T, P])
        x2T = rot_a[:, 0, :]
        sel = sb("sel", [P, T, E])
        selx = sb("selx", [P, T, E])
        top = sb("top", [P, T, 8])
        topi = sb("topi", [P, T, 8], U32)
        topf = sb("topf", [P, T, 8])
        hit = attn[:, :, :, :].rearrange("p t h d -> p (t h d)").rearrange("p (t k e) -> p t k e", t=T, k=TOPK)
        gate = sb("gate", [P, T, E])
        pick32 = gate[0:2 * E, 0, :]
        gateT = sb("gateT", [2 * E, S], FR)
        hid = prob[:, 0:3, :]
        hid_hi = (u_hi[:, 0, 0, :], u_hi[:, 0, 1, :], u_hi[:, 1, 0, :])
        hid_lo = (u_hi[:, 0, 2, :], u_hi[:, 0, 3, :], u_hi[:, 1, 1, :])
        x2_hi, x2_lo = u_hi[:, 1, 2, :], u_hi[:, 1, 3, :]
        moeT = oT

        ps_turn = ps("ps_turn", [P, 2, S])
        ps_guard = ps("ps_guard", [P, 2, S])
        ps_score = ps("ps_score", [P, 2, S])
        ps_acc = ps("ps_acc", [P, 2, S])
        acc, mis = ps_acc[:, 0, :], ps_acc[:, 1, :]

        names = ("w_in x_in setup_pe setup_dve w_spilled w_turned dve_order xn_ready z_ready xnT_ps zT_ps xnT_ready "
                 "xfT_ready proj_ps proj_hi proj_done y_ready qk_spilled q_turned kq0 kq1 kq2 kq3 turn_ps rot_done "
                 "u_sum u_hi_done u_lo_done guard_ps max_done maxT_ps maxT_done row_out row_in score_ps exp_done pv_done "
                 "oT_done oTT_ps attn_done mg_ps mmax_done mmaxT_ps mmaxT_done mainrow_out mainrow_in main_done attnT_ps "
                 "attnT_ready wo_ps src2_ready z2T_ps vm_done x2T_ready x2_hi_done x2_lo_done hid_hi_done hid_lo_done keys_in vals_in0 vals_in1 vals_in2 vals_in3 weights_hi weights_lo low_spilled keys_lo_in0 keys_lo_in1 vals_lo_in3 vals_lo_in4 vals_lo_in5 vals_lo_in6 vals_lo_in7 logit_ps logit_ready esel_done gate_ready gateT_ps gateT_hi gateT_done "
                 "hid_ps relu_done gsel_ps hg_done moe_done moeT_ready moeTT_ps fvar_ready fvar_eps frstd_ready bvar_ready bvar_eps brstd_ready final_ready silu_in esig_done batch_done stored half_set x_free memset_done").split()
        s = {n: sem(n) for n in names}
        s_vals_in = [s[f"vals_in{i}"] for i in range(NC // 2)]
        s_kq = [s[f"kq{i}"] for i in range(NQ)]
        per = dict(x_in=16, xn_ready=1, z_ready=1, xnT_ps=1, zT_ps=1, xnT_ready=1, xfT_ready=1,
                   proj_ps=6, proj_hi=2, proj_done=3, y_ready=1, qk_spilled=64, q_turned=16 * 12, kq=64,
                   turn_ps=2 * H, rot_done=2 * H, u_sum=H, u_hi_done=H, u_lo_done=H, guard_ps=NT, max_done=NT,
                   maxT_ps=NQ, maxT_done=NQ, row_in=16 * NQ, row_out=16 * NQ, mainrow_out=16, score_ps=NT + T, exp_done=NT + T, pv_done=NQ * T + T,
                   oT_done=NQ, oTT_ps=NQ, attn_done=NQ, mg_ps=T, mmax_done=T + 1, mmaxT_ps=1, mmaxT_done=1,
                   mainrow_in=16, main_done=1, attnT_ps=1, attnT_ready=1, wo_ps=1, src2_ready=1, z2T_ps=1,
                   x2T_ready=1, x2_hi_done=1, x2_lo_done=1, hid_hi_done=E, hid_lo_done=E, lo_in=16, logit_ps=1, logit_ready=1, esel_done=1, gate_ready=1, gateT_ps=1, gateT_hi=1, gateT_done=1,
                   hid_ps=E, relu_done=E, gsel_ps=E, hg_done=E, moe_done=E, moeT_ready=1, moeTT_ps=1,
                   final_ready=1, fvar_ready=2, fvar_eps=2, frstd_ready=2, bvar_ready=1, bvar_eps=1, brstd_ready=1, vm_done=2, silu_in=1, esig_done=1, batch_done=1, stored=16, x_free=1)
        FLINK, NLINK = 2, 21
        NW = 28 * 16

        block = ctx.enter_context(nc.Block())

        def main_slot(jb):
            return jb

        def bank_of(n):
            return n % 2

        def pslot(n):
            return (n + T) % PSLOTS

        @block.sync
        def _(eng):
            def load(dst, src):
                eng.dma_start(dst, src).then_inc(s["w_in"], 16)

            eng.dma_start(xin[:, :, :], x[0].rearrange("(t p) d -> p t d", p=P)).then_inc(s["x_in"], 16)
            for dst, src in ((WqA, Wq), (WkA, Wk), (WvA, Wv)):
                load(dst[:, :, :], src.rearrange("(c p) d -> p c d", p=P))
            load(WoA, Wo)
            load(ident[:, :], c_ident)
            for n, src in enumerate((bq, bk, bv)):
                for c in range(2):
                    load(biasA[:, n, c:c + 1], src.rearrange("(c p o) -> c p o", c=2, o=1)[c])
            load(bo_row, bo.partition_broadcast(P))
            for dst, src in ((wqF, wq), (wkF, wk), (wvF, wv), (woF, wo), (selF, sel_w)):
                load(dst[:, :], src)
            for n, src in enumerate((ln1_g, ln1_b, ln2_g, ln2_b)):
                load(lnF[:, n:n + 1], src.rearrange("(p o) -> p o", o=1))
            load(wpF, wp)
            load(span, c_span)
            load(cosT[:, :], c_cos)
            load(sinT[:, :], c_sin)
            load(key_table, c_key)
            load(pick32, c_pick)
            load(iota[:, :, :], c_iota.rearrange("p (k e) -> p k e", k=TOPK))
            eng.dma_start(prob[:, :, :].rearrange("p c (e h) -> p (c e) h", h=P), keys.rearrange("e d h -> d e h"))\
                .then_inc(s["keys_in"], 16)

            eng.wait_ge(s["setup_dve"], 6)
            eng.dma_start(spill_w[0], w_hi.bitcast(F32)).then_inc(s["w_spilled"], 16)
            eng.dma_start(spill_w[1], w_lo.bitcast(F32)).then_inc(s["w_spilled"], 16)
            eng.wait_ge(s["w_spilled"], 32)
            for g in range(QH):
                for r, part in enumerate((0, 0, 1)):
                    src = spill_w[part].rearrange("(q g d) n -> g d q n", g=QH, d=HD)[g]
                    eng.dma_start(turn_w[32 * g + HD * r:32 * g + HD * (r + 1), :, :].bitcast(F32), src)\
                       .then_inc(s["w_turned"], 16)

            def load_vals_lo(b, c):
                eng.wait_ge(s["moe_done"], b * per["moe_done"] + CE * (c - QH + 1))
                eng.dma_start(u_lo[:, 0, c % QH, :].bitcast(F32), low_vals[:, c, :])\
                    .then_inc(s[f"vals_lo_in{c}"], 16)

            def front(b, beside):
                def wait(name, k):
                    eng.wait_ge(s[name], b * per[name] + k)

                if beside:
                    load_vals_lo(b - 1, QH)
                    load_vals_lo(b - 1, QH + 1)
                wait("proj_done", 2)
                for n, src in enumerate((q_hi, q_lo, k_hi, k_lo)):
                    eng.dma_start(spill[n], src.bitcast(F32)).then_inc(s["qk_spilled"], 16)
                wait("qk_spilled", 64)
                for g in range(QH):
                    for r, part in enumerate((0, 1, 0)):
                        src = spill[part].rearrange("(q g d) i -> g d q i", g=QH, d=HD)[g]
                        eng.dma_start(turn_q[32 * g + HD * r:32 * g + HD * (r + 1), :, :].bitcast(F32), src)\
                           .then_inc(s["q_turned"], 16)
                if beside:
                    load_vals_lo(b - 1, QH + 2)
                for q in range(USLOTS):
                    quad_rows(q, ((k_hi4, 2), (k_lo4, 3)))
                if beside:
                    load_vals_lo(b - 1, QH + 3)
                    eng.wait_ge(s["moe_done"], b * per["moe_done"])
                else:
                    eng.wait_ge(s["low_spilled"], 32)
                for q in range(USLOTS):
                    quad_rows(q, ((u_hi, 0), (u_lo, 1)))

            def quad_rows(q, parts):
                for dst, part in parts:
                    src = spill[part].rearrange("(q g d) i -> q d g i", g=QH, d=HD)[q]
                    eng.dma_start(dst[RF:RQ, q % USLOTS, :, :].bitcast(F32), src).then_inc(s_kq[q], 16)

            def batch(b, more):
                def wait(name, k):
                    eng.wait_ge(s[name], b * per[name] + k)

                def guard_row(q):
                    wait("maxT_done", q + 1)
                    eng.dma_start(spill_row[q], rowmaxT[:, q % 2, :].bitcast(F32)).then_inc(s["row_out"], 16)
                    wait("row_out", 16 * (q + 1))
                    eng.dma_start(u_hi[RQ:RK, q % USLOTS, :, :].bitcast(F32),
                                  spill_row[q].rearrange("(o g t) i -> o g (t i)", o=1, g=QH)).then_inc(s["row_in"], 16)

                if more:
                    wait("x_free", 1)
                    load_x(b + 1)
                wait("mmaxT_done", 1)
                eng.dma_start(spill_main, mainrowT[:, :].bitcast(F32)).then_inc(s["mainrow_out"], 16)
                wait("mainrow_out", 16)
                eng.dma_start(mainrow.bitcast(F32), spill_main.rearrange("(o t) i -> o (t i)", o=1))\
                    .then_inc(s["mainrow_in"], 16)
                guard_row(0)
                guard_row(1)
                wait("score_ps", T + 16 * (NQ - USLOTS))
                quad_rows(NQ - 1, ((u_hi, 0), (u_lo, 1), (k_hi4, 2), (k_lo4, 3)))
                guard_row(2)
                for u in range(2):
                    wait("score_ps", T + 16 * (u + 2))
                    eng.dma_start(u_lo[:, 1 + u, :, :].bitcast(F32), low_keys[:, QH * u:QH * u + QH, :])\
                        .then_inc(s[f"keys_lo_in{u}"], 16)
                    if u == 0:
                        guard_row(3)
                wait("score_ps", T + NT)
                eng.dma_start(u_lo[:, 0, :, :].bitcast(F32), low_vals[:, 0:QH, :])\
                    .then_inc(s[f"vals_lo_in{QH - 1}"], 16)
                if more:
                    front(b + 1, True)
                else:
                    for c in range(QH, NC):
                        load_vals_lo(b, c)
                wait("batch_done", 2)
                eng.dma_start(out[b].rearrange("(t p) d -> p t d", p=P), res[:, :, :]).then_inc(s["stored"], 16)

            def load_x(b):
                eng.dma_start(xin[:, :, :], x[b].rearrange("(t p) d -> p t d", p=P)).then_inc(s["x_in"], 16)

            for c in range(0, NC, 2):
                eng.wait_ge(s["weights_lo"], c + 2)
                eng.dma_start(prob[:, c:c + 2, :].rearrange("p c (e h) -> p (c e) h", h=P),
                              values[CE * c:CE * c + 2 * CE].rearrange("e h d -> h e d"))\
                    .then_inc(s_vals_in[c // 2], 16)
            eng.dma_start(low_keys, keys_low_stage.bitcast(F32)).then_inc(s["low_spilled"], 16)
            eng.wait_ge(s["weights_lo"], 2 * NC)
            eng.dma_start(low_vals, vals_low_stage.bitcast(F32)).then_inc(s["low_spilled"], 16)
            front(0, False)
            with eng.Fori(0, B - 1) as b:
                batch(b, True)
            batch(B - 1, False)
            eng.wait_ge(s["stored"], 16 * (B + 1))

        @block.tensor
        def _(eng):
            mm, tr = eng.matmul, eng.transpose
            eng.wait_ge(s["w_in"], NW)
            for c in range(2):
                tr(ps_turn[:, 0, c * P:(c + 1) * P], WoA[:, c * P:(c + 1) * P], ident[:, :])
            tail = mm(ps_turn[:, 1, 0:2 * RF], wpF, span, start=True, stop=True)
            tail.then_inc(s["setup_pe"], 1)
            eng.wait_ge(s["setup_dve"], 1)
            for c in range(2):
                mm(ps_score[:, 0, 0:P], WqA[:, c, :], WkA[:, c, :], start=c == 0, stop=c == 1)
            for c in range(2):
                mm(ps_score[:, 1, 0:P], WvA[:, c, :], WoT[:, c, :], start=c == 0, stop=c == 1)
            for c in range(2):
                mm(ps_guard[:, 0, 0:1], WkA[:, c, :], biasA[:, 0, c:c + 1], start=c == 0, stop=c == 1)
            for c in range(2):
                mm(ps_guard[:, 1, 0:1], WqA[:, c, :], biasA[:, 1, c:c + 1], start=c == 0, stop=c == 1)
            for c in range(2):
                mm(mis[:, 0:1], biasA[:, 0, c:c + 1].to_broadcast([P, P]), biasA[:, 1, c:c + 1],
                   start=c == 0, stop=c == 1)
            for c in range(2):
                tail = mm(acc[:, 0:P], biasA[:, 2, c:c + 1].to_broadcast([P, P]), WoT[:, c, :],
                          start=c == 0, stop=c == 1)
            tail.then_inc(s["setup_pe"], 1)
            eng.wait_ge(s["setup_dve"], 12)
            eng.wait_ge(s["w_turned"], 12 * 16)

            def front(b, at):
                def wait(name, k):
                    eng.wait_ge(s[name], b * per[name] + k)

                def values_main(c):
                    for t in range(2 * c, 2 * c + 2):
                        tail = mm(ps_turn[:, 1 - c, (t % 2) * (P + 1):(t % 2 + 1) * (P + 1)],
                                  xnT[:, t * P:(t + 1) * P], wvo[:, :], start=t % 2 == 0, stop=t % 2 == 1,
                                  skip_group_check=True)
                    tail.then_inc(s["proj_ps"], 1)

                if at == PE_XN:
                    wait("xn_ready", 1)
                    for t in range(T):
                        tail = tr(ps_turn[:, 0, t * P:(t + 1) * P], xn[:, t, :], ident[:, :])
                    tail.then_inc(s["xnT_ps"], 1)
                if at == PE_Z:
                    wait("z_ready", 1)
                    for t in range(T):
                        tail = tr(ps_turn[:, 1, t * P:(t + 1) * P], zn[:, t, :], ident[:, :])
                    tail.then_inc(s["zT_ps"], 1)
                if at == PE_QK:
                    wait("xnT_ready", 1)
                    wait("xfT_ready", 1)
                    mm(ps_turn[:, 0, :], wqF[:, :], xfT[:, :], start=True, stop=True).then_inc(s["proj_ps"], 1)
                    mm(ps_turn[:, 1, :], wkF[:, :], xfT[:, :], start=True, stop=True).then_inc(s["proj_ps"], 1)
                if at == PE_Y:
                    wait("proj_done", 1)
                    mm(ps_turn[:, 0, :], wqk[:, :], xnT[:, :], start=True, stop=True).then_inc(s["proj_ps"], 1)
                    wait("proj_done", 2)
                    values_main(0)
                if at == PE_V:
                    wait("y_ready", 1)
                    values_main(1)
                    wait("vm_done", 1)
                    for t in range(T):
                        tail = mm(ps_turn[:, 1, t * P:(t + 1) * P], xfT[:, t * P:(t + 1) * P], wvF[:, :],
                                  start=t == 0, stop=t == T - 1, skip_group_check=True)
                    tail.then_inc(s["proj_ps"], 1)

            def batch(b, more):
                def wait(name, k):
                    eng.wait_ge(s[name], b * per[name] + k)

                for tick in range(TICKS):
                    m = tick - MAIN_GUARD
                    if 0 <= m < T:
                        if m == 0:
                            wait("y_ready", 1)
                        if m >= 2:
                            wait("mmax_done", m - 1)
                        mm(ps_score[:, m % 2, :], yT[:, m * P:(m + 1) * P], xnT[:, :],
                           start=True, stop=True).then_inc(s["mg_ps"], 1)
                    if tick == MAIN_ROW:
                        wait("mmax_done", T + 1)
                        tr(mis[0:T, 0:P], mmax[:, 2, :], ident[:, :]).then_inc(s["mmaxT_ps"], 1)
                    m = (tick - MAIN_SCORE)
                    if 0 <= m < 2 * T and m % 2 == 0:
                        jb = m // 2
                        if jb == 0:
                            wait("mainrow_in", 16)
                        if jb >= 2:
                            wait("exp_done", jb - 1)
                        mm(ps_score[:, jb % 2, :], xnT[:, jb * P:(jb + 1) * P], yT[:, :], start=True, stop=False)
                        mm(ps_score[:, jb % 2, :], ones_row[:, :], mainrow, start=False, stop=True)\
                            .then_inc(s["score_ps"], 1)
                    if 2 <= m < 2 * T + 2 and m % 2 == 0:
                        jb = m // 2 - 1
                        wait("exp_done", jb + 1)
                        for ib in range(T):
                            tail = mm(ps_acc[:, ib // 2, (ib % 2) * (P + 1):(ib % 2 + 1) * (P + 1)],
                                      prob[:, main_slot(jb), ib * P:(ib + 1) * P], vmain[:, jb, :],
                                      start=jb == 0 and ib % 2 == 0, stop=jb == T - 1 and ib % 2 == 1,
                                      skip_group_check=True)
                        tail.then_inc(s["pv_done"], 1)

                    if tick % 4 == 0 and tick // 4 < H:
                        h = tick // 4
                        g = h % QH
                        if h == 0:
                            wait("q_turned", 12 * 16)
                            wait("vm_done", 2)
                            wait("proj_done", 3)
                        if h >= 1:
                            wait("rot_done", 2 * h - 1)
                        rows = slice(32 * g, 32 * g + 3 * HD)
                        mm(ps_turn[0:RF, 0, :], turn_w[rows, h // QH, 0:RF], turn_q[rows, h // QH, :],
                           start=True, stop=True).then_inc(s["turn_ps"], 1)
                        if h >= 1:
                            wait("rot_done", 2 * h)
                        mm(ps_turn[0:RF, 1, :], turn_w[rows, h // QH, RF:2 * RF], turn_q[rows, h // QH, :],
                           start=True, stop=True).then_inc(s["turn_ps"], 1)
                    n = tick - SCORE_AT
                    if 0 <= n < NT:
                        q, jb, g = n // 16, n // 4 % 4, n % 4
                        slot = q % USLOTS
                        if n % 16 == 0:
                            wait("u_lo_done", QH * (q + 1))
                            wait("row_in", 16 * (q + 1))
                        wait("exp_done", T + n - 1)
                        ko = slice(jb * P, (jb + 1) * P)
                        o = ps_score[:, bank_of(n), :]
                        mm(o, k_hi4[0:RK, slot, g, ko], u_hi[0:RK, slot, g, :], start=True, stop=False)
                        mm(o, k_hi4[0:RQ, slot, g, ko], u_lo[0:RQ, slot, g, :], start=False, stop=False)
                        mm(o, k_lo4[0:RK, slot, g, ko], u_hi[0:RK, slot, g, :], start=False, stop=True)\
                            .then_inc(s["score_ps"], 1)
                    n = tick - GUARD_AT
                    if 0 <= n < NT:
                        h, ib = n // T, n % T
                        q, g = h // QH, h % QH
                        if ib == 0:
                            wait("u_hi_done", h + 1)
                        if n % 16 == 0:
                            eng.wait_ge(s_kq[q], b * per["kq"] + 64)
                        if n >= 2:
                            wait("max_done", n - 1)
                        mm(ps_guard[:, n % 2, :], u_hi[0:RQ, q % USLOTS, g, ib * P:(ib + 1) * P],
                           k_hi4[0:RQ, q % USLOTS, g, :], start=True, stop=True).then_inc(s["guard_ps"], 1)
                    n = tick - GUARD_AT - 16
                    if n >= 0 and n % 16 == 0 and n // 16 < NQ:
                        q = n // 16
                        wait("max_done", 16 * (q + 1))
                        if q == 0:
                            wait("main_done", 1)
                        else:
                            wait("maxT_done", q)
                        if q >= 2:
                            wait("attn_done", q - 1)
                        tr(mis[0:QH * T, 0:P], rowmax[:, q % 2, :], ident[:, :]).then_inc(s["maxT_ps"], 1)
                    n = tick - SCORE_AT - 6
                    if n >= 0 and n % 4 == 0 and n // 4 < NQ * T:
                        m = n // 4
                        q, jb = m // T, m % T
                        wait("exp_done", T + 4 * (m + 1))
                        if jb == 0:
                            if q == 0:
                                wait("main_done", 1)
                            else:
                                wait("oT_done", q)
                        for g in range(QH):
                            c = (QH * q + g) * (HD + 1)
                            tail = mm(acc[32 * g:32 * g + 32, :], vhead[:, jb, c:c + 32],
                                      prob[:, pslot(4 * m + g), :], start=jb == 0, stop=jb == T - 1)
                        tail.then_inc(s["pv_done"], 1)
                    n = tick - SCORE_AT - 21
                    if n >= 0 and n % 16 == 0 and n // 16 < NQ:
                        q = n // 16
                        wait("oT_done", q + 1)
                        wait("maxT_done", min(q + 2, NQ))
                        if q >= 1:
                            wait("attn_done", q)
                        for t in range(T):
                            tail = tr(mis[:, t * P:(t + 1) * P], oT[:, t * P:(t + 1) * P], ident[:, :])
                        tail.then_inc(s["oTT_ps"], 1)

                wait("attn_done", NQ)
                for t in range(T):
                    tail = tr(mis[:, t * P:(t + 1) * P], attn[:, t, :, :].rearrange("p h d -> p (h d)"), ident[:, :])
                tail.then_inc(s["attnT_ps"], 1)
                wait("attnT_ready", 1)
                for t in range(T):
                    tail = mm(acc[:, t * P:(t + 1) * P], attnT[:, t * P:(t + 1) * P], woF[:, :],
                              start=t == 0, stop=t == T - 1, skip_group_check=True)
                tail.then_inc(s["wo_ps"], 1)
                wait("src2_ready", 1)
                for t in range(T):
                    tail = tr(mis[:, t * P:(t + 1) * P], zn[:, t, :], ident[:, :])
                tail.then_inc(s["z2T_ps"], 1)
                wait("x2T_ready", 1)
                for t in range(T):
                    tail = mm(acc[:, t * E:(t + 1) * E], x2T[:, t * P:(t + 1) * P], selF[:, :],
                              start=t == 0, stop=t == T - 1, skip_group_check=True)
                tail.then_inc(s["logit_ps"], 1)

                def hidden(e):
                    if e >= 2:
                        wait("relu_done", e - 1)
                    if e % (E // 2) == 0:
                        eng.wait_ge(s[f"keys_lo_in{e // (E // 2)}"], b * per["lo_in"] + 16)
                    o = ps_score[:, e % 2, :]
                    mm(o, keys_hi[:, e, :], x2_hi, start=True, stop=False)
                    mm(o, keys_lo(e), x2_hi, start=False, stop=False)
                    if e == 0:
                        wait("x2_lo_done", 1)
                    mm(o, keys_hi[:, e, :], x2_lo, start=False, stop=True).then_inc(s["hid_ps"], 1)

                wait("x2_hi_done", 1)
                hidden(0)
                hidden(1)
                wait("gate_ready", 1)
                for t in range(T):
                    tail = tr(mis[0:E, t * P:(t + 1) * P], gate[:, t, :], ident[:, :])
                tail.then_inc(s["gateT_ps"], 1)
                wait("gateT_done", 1)
                for e in range(E + LAG):
                    if more:
                        front(b + 1, e)
                    if e < E:
                        if e >= 2:
                            hidden(e)
                            wait("hg_done", e - 1)
                        mm(ps_guard[:, e % 2, :], pick[:, e:e + 1].to_broadcast([2 * E, P]), gateT[:, :],
                           start=True, stop=True).then_inc(s["gsel_ps"], 1)
                    if e >= LAG:
                        f = e - LAG
                        if f % CE == 0 and (f == 0 or f >= QH * CE):
                            eng.wait_ge(s[f"vals_lo_in{max(f // CE, QH - 1)}"], b * per["lo_in"] + 16)
                        wait("hid_hi_done", f + 1)
                        if f == 0:
                            wait("logit_ready", 1)
                        mm(acc, vals_hi[:, f, :], hid_hi[f % 3], start=f == 0, stop=False)
                        mm(acc, vals_lo(f), hid_hi[f % 3], start=False, stop=False)
                        wait("hid_lo_done", f + 1)
                        mm(acc, vals_hi[:, f, :], hid_lo[f % 3], start=False, stop=f == E - 1)\
                            .then_inc(s["moe_done"], 1)
                wait("moeT_ready", 1)
                for t in range(T):
                    tail = tr(mis[:, t * P:(t + 1) * P], moeT[:, t * P:(t + 1) * P], ident[:, :])
                tail.then_inc(s["moeTT_ps"], 1)

            for at in range(E):
                front(0, at)
            with eng.Fori(0, B - 1) as b:
                batch(b, True)
            batch(B - 1, False)

        @block.vector
        def _(eng):
            V = eng

            def setup(ins):
                ins.then_inc(s["setup_dve"], 1)

            V.memset(k_hi4[96:P, :, :, :].bitcast(F32), 1.0).then_inc(s["memset_done"], 1)
            V.memset(k_lo4[96:P, :, :, :].bitcast(F32), 0.0).then_inc(s["memset_done"], 1)
            V.memset(vhead[:, :, :], 1.0).then_inc(s["memset_done"], 1)
            V.memset(vmain[:, :, :], 1.0).then_inc(s["memset_done"], 1)
            V.memset(ones_row[:, :].bitcast(F32), 1.0).then_inc(s["memset_done"], 1)
            V.wait_ge(s["memset_done"], 5)
            V.wait_ge(s["w_in"], NW)
            V.wait_ge(s["setup_pe"], 1)
            setup(V.tensor_copy(WoT[:, :, :], ps_turn[:, 0, 0:2 * P].rearrange("p (c n) -> p c n", c=2)))
            setup(V.tensor_copy(w_hi, ps_turn[:, 1, 0:2 * RF]))
            setup(V.tensor_copy(k_hi4[0:RF, 0, 0, :], key_table))
            setup(V.tensor_copy(pick[:, :], pick32))
            V.wait_ge(s["setup_dve"], 4)
            setup(V.tensor_tensor(w_lo, ps_turn[:, 1, 0:2 * RF], w_hi.bitcast(F32), ALU.subtract))
            setup(V.tensor_tensor(k_lo4[0:RF, 0, 0, :], key_table, k_hi4[0:RF, 0, 0, :].bitcast(F32),
                                  ALU.subtract))
            V.wait_ge(s["setup_dve"], 6)
            for i in range(1, USLOTS * QH):
                V.tensor_copy(k_hi4[0:RF, i // QH, i % QH, :], k_hi4[0:RF, 0, 0, :].bitcast(F32))
                V.tensor_copy(k_lo4[0:RF, i // QH, i % QH, :], k_lo4[0:RF, 0, 0, :].bitcast(F32))
            V.wait_ge(s["setup_pe"], 2)
            setup(V.tensor_copy(wqk[:, :], ps_score[:, 0, 0:P]))
            setup(V.tensor_copy(wvo[:, 0:P], ps_score[:, 1, 0:P]))
            setup(V.tensor_copy(y_bias[:, :], ps_guard[:, 0, 0:1]))
            setup(V.tensor_copy(wvo[:, P:P + 1], ps_guard[:, 1, 0:1]))
            setup(V.tensor_copy(bqbk[:, :], mis[:, 0:1]))
            setup(V.tensor_tensor(out_bias[:, :], acc[:, 0:P], bo_row, ALU.add))
            V.wait_ge(s["setup_dve"], 12)
            V.memset(carrier[:, :], 0.0).then_inc(s["batch_done"], 1)
            V.memset(rhead[:, :, :], 0.0).then_inc(s["stored"], 16)

            links, chain = [0], [0]

            def link(ins, fixed=False):
                links[0] += 1
                ins.then_inc(s["dve_order"], 1)
                eng.wait_ge(s["dve_order"], chain[0] + links[0])
                if fixed:
                    V.memset(carrier[:, :], 0.0)

            def norm_stats(src):
                for t in range(T):
                    i = V.bn_stats(stats[:, t, :], src[:, t, :])
                link(i, fixed=True)

            def norm_mean(ready):
                for t in range(T):
                    i = V.bn_aggr(mv[:, t, :], stats[:, t, :])
                i.then_inc(s[ready], 1)

            def norm_apply(dst, src, done):
                for t in range(T):
                    i = V.tensor_scalar(dst[:, t, :], src[:, t, :], mv[:, t, 0:1], rstd[:, t:t + 1],
                                        ALU.subtract, ALU.mult)
                i.then_inc(s[done], 1)

            def front(b, at):
                def wait(name, k):
                    eng.wait_ge(s[name], b * per[name] + k)

                def values_main(c):
                    wait("proj_ps", 4 + c)
                    pv = ps_turn[:, 1 - c, 0:2 * (P + 1)].rearrange("p (t n) -> p t n", t=2)
                    V.tensor_copy(vmain[:, 2 * c:2 * c + 2, 0:P], pv[:, :, 0:P])
                    return V.tensor_scalar(cmain[:, 2 * c:2 * c + 2], pv[:, :, P], bqbk[:, 0:1], None, ALU.add)\
                        .then_inc(s["vm_done"], 1)

                if at == V_STATS1:
                    wait("x_in", 16)
                    norm_stats(xin)
                if at == V_MEAN1:
                    norm_mean("fvar_ready")
                if at == V_NORM1:
                    wait("frstd_ready", 1)
                    norm_apply(xn, xin, "xn_ready")
                if at == V_STATS2:
                    wait("xn_ready", 1)
                    V.memset(carrier[:, :], 0.0)
                    norm_stats(xn)
                if at == V_MEAN2:
                    norm_mean("fvar_ready")
                if at == V_NORM2:
                    wait("frstd_ready", 2)
                    norm_apply(zn, xn, "z_ready")
                if at == V_Z:
                    wait("zT_ps", 1)
                    V.tensor_scalar(xfT[:, :], ps_turn[:, 1, :], lnF[:, 0:1], lnF[:, 1:2], ALU.mult, ALU.add)\
                        .then_inc(s["xfT_ready"], 1)
                if at == V_QK:
                    for n, (lo, hi) in enumerate(((q_lo, q_hi), (k_lo, k_hi))):
                        wait("proj_hi", n + 1)
                        V.tensor_tensor(lo, ps_turn[:, n, :], hi.bitcast(F32), ALU.subtract)\
                            .then_inc(s["proj_done"], 1)
                if at == V_VM0:
                    values_main(0)
                if at == V_VM1:
                    values_main(1)
                if at == V_VHEAD:
                    wait("proj_ps", 6)
                    V.tensor_copy(vhead[:, :, 0:H * (HD + 1)].rearrange("p t (h c) -> p t h c", h=H)[:, :, :, 0:HD],
                                  ps_turn[:, 1, :].rearrange("p (t h c) -> p t h c", t=T, h=H))\
                        .then_inc(s["proj_done"], 1)

            def batch(b, more):
                def wait(name, k):
                    eng.wait_ge(s[name], b * per[name] + k)

                links[0], chain[0] = 0, b * NLINK + FLINK
                wait("batch_done", 1)
                V.tensor_copy(xres[:, :, :], xin[:, :, :]).then_inc(s["x_free"], 1)

                for tick in range(TICKS):
                    m = tick - MAIN_GUARD
                    if 0 <= m < T:
                        wait("mg_ps", m + 1)
                        V.tensor_reduce(mmax[:, 0, m:m + 1], ps_score[:, m % 2, :], X, ALU.max)\
                            .then_inc(s["mmax_done"], 1)
                    if tick == T - 1:
                        wait("mmax_done", T)
                        wait("vm_done", 2)
                        link(V.tensor_tensor(mmax[:, 1, :], mmax[:, 0, :], cmain[:, :], ALU.add))
                        V.tensor_tensor(mmax[:, 2, :], cmain[:, :], mmax[:, 1, :], ALU.subtract)\
                            .then_inc(s["mmax_done"], 1)
                    if tick == MAIN_OUT:
                        wait("pv_done", T)
                        for c in range(2):
                            pa = ps_acc[:, c, 0:2 * (P + 1)].rearrange("p (t n) -> p t n", t=2)
                            i = V.reciprocal(rmain[:, 2 * c:2 * c + 2], pa[:, :, P])
                        link(i)
                        for t in range(T):
                            o = (t % 2) * (P + 1)
                            i = V.scalar_tensor_tensor(smain[:, t, :], ps_acc[:, t // 2, o:o + P], rmain[:, t:t + 1],
                                                       out_bias[:, :], ALU.mult, ALU.add)
                        i.then_inc(s["main_done"], 1)
                    n = tick - GUARD_AT
                    if 0 <= n < NT:
                        q = n // 16
                        if n % 16 == 0 and q >= 2:
                            wait("maxT_ps", q - 1)
                        wait("guard_ps", n + 1)
                        V.tensor_reduce(rowmax[:, q % 2, n % 16:n % 16 + 1], ps_guard[:, n % 2, :], X, ALU.max)\
                            .then_inc(s["max_done"], 1)
                    if tick % 4 == 0 and tick // 4 < H:
                        h = tick // 4
                        if h >= 2:
                            wait("u_lo_done", h - 1)
                        wait("turn_ps", 2 * h + 1)
                        V.tensor_tensor(rot_a[0:RF, h % 2, :], ps_turn[0:RF, 0, :], cosT[:, :], ALU.mult)\
                            .then_inc(s["rot_done"], 1)
                        wait("turn_ps", 2 * h + 2)
                        V.tensor_tensor(rot_b[0:RF, h % 2, :], ps_turn[0:RF, 1, :], sinT[:, :], ALU.mult)\
                            .then_inc(s["rot_done"], 1)
                    n = tick - SCORE_AT - 22
                    if n >= 0 and n % 16 == 0 and n // 16 < NQ:
                        q = n // 16
                        wait("oTT_ps", q + 1)
                        pt = mis.rearrange("p (t g r) -> p t g r", t=T, g=QH)
                        link(V.reciprocal(rhead[:, :, :], pt[:, :, :, HD]))
                        V.tensor_tensor(attn[:, :, QH * q:QH * q + QH, :], pt[:, :, :, 0:HD],
                                        rhead[:, :, :].unsqueeze(3).to_broadcast([P, T, QH, HD]), ALU.mult)\
                            .then_inc(s["attn_done"], 1)

                wait("wo_ps", 1)
                link(V.tensor_tensor(src2[:, :, :], acc.rearrange("p (t d) -> p t d", t=T), xn[:, :, :], ALU.add))
                norm_stats(src2)
                norm_mean("bvar_ready")
                wait("brstd_ready", 1)
                norm_apply(zn, src2, "src2_ready")
                wait("z2T_ps", 1)
                V.tensor_scalar(x2T, mis, lnF[:, 2:3], lnF[:, 3:4], ALU.mult, ALU.add)\
                    .then_inc(s["x2T_ready"], 1)
                wait("logit_ps", 1)
                V.tensor_scalar(selx[:, :, :], acc[:, 0:T * E].rearrange("p (t e) -> p t e", t=T), -87.0, None,
                                ALU.max).then_inc(s["logit_ready"], 1)
                wait("esel_done", 1)
                link(V.tensor_scalar(selx[:, :, :], sel[:, :, :], 1.0, None, ALU.add))
                link(V.reciprocal(sel[:, :, :], selx[:, :, :]), fixed=True)
                for t in range(T):
                    i = V.max(top[:, t, :], sel[:, t, :])
                link(i, fixed=True)
                for t in range(T):
                    i = V.max_index(topi[:, t, :], top[:, t, :], sel[:, t, :])
                link(i)
                link(V.tensor_copy(topf[:, :, :], topi[:, :, :]))
                for t in range(T):
                    i = V.tensor_tensor(hit[:, t, :, :], iota[:, :, :],
                                        topf[:, t, 0:TOPK].unsqueeze(2).to_broadcast([P, TOPK, E]), ALU.is_equal)
                link(i)
                link(V.tensor_reduce(selx[:, :, :], hit[:, :, :, :].rearrange("p t k e -> p t e k"), X, ALU.add))
                V.tensor_tensor(gate[:, :, :], sel[:, :, :], selx[:, :, :], ALU.mult).then_inc(s["gate_ready"], 1)
                wait("gateT_hi", 1)
                V.tensor_tensor(gateT[E:2 * E, :], mis[0:E, :], gateT[0:E, :].bitcast(F32), ALU.subtract)\
                    .then_inc(s["gateT_done"], 1)

                for e in range(E):
                    if more:
                        front(b + 1, e)
                    wait("relu_done", e + 1)
                    wait("gsel_ps", e + 1)
                    V.tensor_tensor(hid[:, e % 3, :], ps_guard[:, e % 2, :], hid[:, e % 3, :], ALU.mult)\
                        .then_inc(s["hg_done"], 1)

                tmp = attn[:, :, :, :].rearrange("p t h d -> p t (h d)")
                wait("moeTT_ps", 1)
                V.tensor_tensor(src2[:, :, :], mis.rearrange("p (t d) -> p t d", t=T), src2[:, :, :], ALU.add)\
                    .then_inc(s["final_ready"], 1)
                wait("final_ready", 1)
                V.tensor_scalar(tmp, src2[:, :, :], -87.0, None, ALU.max).then_inc(s["silu_in"], 1)
                link(V.tensor_tensor(src2[:, :, :], src2[:, :, :], smain[:, :, :], ALU.mult))
                wait("esig_done", 1)
                link(V.tensor_scalar(tmp, oT[:, :].rearrange("p (t d) -> p t d", t=T), 1.0, None, ALU.add))
                link(V.reciprocal(smain[:, :, :], tmp))
                link(V.tensor_tensor(tmp, src2[:, :, :], smain[:, :, :], ALU.mult))
                wait("stored", 16)
                V.tensor_tensor(res[:, :, :], tmp, xres[:, :, :], ALU.add).then_inc(s["batch_done"], 1)

                assert not more or links[0] == NLINK, links[0]

            for at in range(E):
                front(0, at)
                if at == V_NORM2:
                    for c in range(NC):
                        V.wait_ge(s["weights_hi"], c + 1)
                        e = slice(CE * c, CE * c + CE)
                        V.tensor_tensor(keys_low_stage[:, c, :], prob[:, c, :],
                                        keys_hi[:, e, :].bitcast(F32).rearrange("p e h -> p (e h)"), ALU.subtract)\
                            .then_inc(s["weights_lo"], 1)
                    for c in range(NC):
                        V.wait_ge(s["weights_hi"], NC + c + 1)
                        e = slice(CE * c, CE * c + CE)
                        V.tensor_tensor(vals_low_stage[:, c, :], prob[:, c, :],
                                        vals_hi[:, e, :].bitcast(F32).rearrange("p e h -> p (e h)"), ALU.subtract)\
                            .then_inc(s["weights_lo"], 1)
            assert links[0] == FLINK, links[0]
            with eng.Fori(0, B - 1) as b:
                batch(b, True)
            batch(B - 1, False)

        @block.scalar
        def _(eng):
            def front(b, at):
                def wait(name, k):
                    eng.wait_ge(s[name], b * per[name] + k)

                if at == ACT_XN:
                    wait("xnT_ps", 1)
                    eng.activation(xnT[:, :], ps_turn[:, 0, :], ACT.Copy).then_inc(s["xnT_ready"], 1)
                if at == ACT_QK:
                    for n, hi in enumerate((q_hi, k_hi)):
                        wait("proj_ps", n + 1)
                        eng.activation(hi, ps_turn[:, n, :], ACT.Copy).then_inc(s["proj_hi"], 1)
                if at == ACT_Y:
                    wait("proj_ps", 3)
                    eng.activation(yT[:, :], ps_turn[:, 0, :], ACT.Identity, bias=y_bias[:, 0:1])\
                        .then_inc(s["y_ready"], 1)

            def batch(b, more):
                def wait(name, k):
                    eng.wait_ge(s[name], b * per[name] + k)

                for tick in range(TICKS):
                    if tick == MAIN_ROW:
                        wait("mmaxT_ps", 1)
                        eng.activation(mainrowT[:, :], mis[0:T, 0:P], ACT.Copy).then_inc(s["mmaxT_done"], 1)
                    m = tick - MAIN_SCORE
                    if 0 <= m < 2 * T and m % 2 == 0:
                        jb = m // 2
                        wait("score_ps", jb + 1)
                        eng.activation(prob[:, main_slot(jb), :], ps_score[:, jb % 2, :], ACT.Exp, scale=MAIN_SCALE)\
                            .then_inc(s["exp_done"], 1)
                    n = tick - SCORE_AT
                    if 0 <= n < NT:
                        m = n // 4
                        wait("score_ps", T + n + 1)
                        if n % 4 == 0:
                            wait("pv_done", T if m < 2 else T + m - 1)
                        eng.activation(prob[:, pslot(n), :], ps_score[:, bank_of(n), :], ACT.Exp, scale=HEAD_SCALE)\
                            .then_inc(s["exp_done"], 1)
                    if tick % 4 == 2 and tick // 4 < H:
                        h = tick // 4
                        q = h // QH
                        wait("u_sum", h + 1)
                        if q >= USLOTS:
                            wait("score_ps", T + 16 * (q - USLOTS + 1))
                        eng.activation(u_hi[0:RF, q % USLOTS, h % QH, :], rot_a[0:RF, h % 2, :], ACT.Copy)\
                            .then_inc(s["u_hi_done"], 1)
                    n = tick - GUARD_AT - 16
                    if n >= 0 and n % 16 == 0 and n // 16 < NQ:
                        q = n // 16
                        wait("maxT_ps", q + 1)
                        if q >= 2:
                            wait("row_in", 16 * (q - 1))
                        eng.activation(rowmaxT[:, q % 2, :], mis[0:QH * T, 0:P], ACT.Copy, scale=-1.0)\
                            .then_inc(s["maxT_done"], 1)
                    n = tick - SCORE_AT - 20
                    if n >= 0 and n % 16 == 0 and n // 16 < NQ:
                        q = n // 16
                        wait("pv_done", T + T * (q + 1))
                        if q >= 1:
                            wait("oTT_ps", q)
                        eng.activation(oT[:, :], acc, ACT.Copy).then_inc(s["oT_done"], 1)

                wait("attnT_ps", 1)
                eng.activation(attnT[:, :], mis, ACT.Copy).then_inc(s["attnT_ready"], 1)
                wait("x2T_ready", 1)
                eng.activation(x2_hi, x2T, ACT.Copy).then_inc(s["x2_hi_done"], 1)
                wait("logit_ready", 1)
                eng.activation(sel[:, :, :], selx[:, :, :], ACT.Exp, scale=-1.0)\
                    .then_inc(s["esel_done"], 1)
                for e in range(E + 1):
                    if more:
                        front(b + 1, e)
                    if e < E:
                        wait("hid_ps", e + 1)
                        if e >= 3:
                            wait("hid_lo_done", e - 2)
                        eng.activation(hid[:, e % 3, :], ps_score[:, e % 2, :], ACT.Relu).then_inc(s["relu_done"], 1)
                    if e == 1:
                        wait("gateT_ps", 1)
                        eng.activation(gateT[0:E, :], mis[0:E, :], ACT.Copy).then_inc(s["gateT_hi"], 1)
                    if e >= 1:
                        f = e - 1
                        wait("hg_done", f + 1)
                        if f >= 3:
                            wait("moe_done", f - 2)
                        eng.activation(hid_hi[f % 3], hid[:, f % 3, :], ACT.Copy).then_inc(s["hid_hi_done"], 1)
                wait("moe_done", E)
                eng.activation(moeT[:, :], acc, ACT.Copy).then_inc(s["moeT_ready"], 1)
                wait("silu_in", 1)
                eng.activation(oT[:, :].rearrange("p (t d) -> p t d", t=T),
                               attn[:, :, :, :].rearrange("p t h d -> p t (h d)"), ACT.Exp, scale=-1.0)\
                    .then_inc(s["esig_done"], 1)

            eng.wait_ge(s["keys_in"], 16)
            for c in range(NC):
                eng.activation(keys_hi[:, CE * c:CE * c + CE, :].rearrange("p e h -> p (e h)"), prob[:, c, :], ACT.Copy)\
                    .then_inc(s["weights_hi"], 1)
            for c in range(NC):
                if c % 2 == 0:
                    eng.wait_ge(s_vals_in[c // 2], 16)
                eng.activation(vals_hi[:, CE * c:CE * c + CE, :].rearrange("p e h -> p (e h)"),
                               prob[:, c, :], ACT.Copy).then_inc(s["weights_hi"], 1)
            for at in range(E):
                front(0, at)
            with eng.Fori(0, B - 1) as b:
                batch(b, True)
            batch(B - 1, False)

        @block.gpsimd
        def _(eng):
            eng.memset(minus_half[:, :], -0.5).then_inc(s["half_set"], 1)
            eng.memset(eps[:, :], EPS).then_inc(s["half_set"], 1)
            eng.wait_ge(s["half_set"], 2)
            def root(b, side, n):
                def wait(name, k):
                    eng.wait_ge(s[name], b * per[name] + k)

                wait(side + "var_ready", n)
                eng.tensor_tensor(var_eps[:, :], mv[:, :, 1], eps[:, :], ALU.add).then_inc(s[side + "var_eps"], 1)
                wait(side + "var_eps", n)
                eng.tensor_tensor(rstd[:, :], var_eps[:, :], minus_half[:, :], ALU.pow)\
                   .then_inc(s[side + "rstd_ready"], 1)

            def batch(b, more):
                def wait(name, k):
                    eng.wait_ge(s[name], b * per[name] + k)

                def add(h):
                    wait("rot_done", 2 * h + 2)
                    eng.tensor_tensor(rot_a[0:RF, h % 2, :], rot_a[0:RF, h % 2, :], rot_b[0:RF, h % 2, :], ALU.add)\
                       .then_inc(s["u_sum"], 1)

                def low(h):
                    q = h // QH
                    wait("u_hi_done", h + 1)
                    if q >= USLOTS:
                        wait("score_ps", T + 16 * (q - USLOTS + 1))
                    eng.tensor_tensor(u_lo[0:RF, q % USLOTS, h % QH, :], rot_a[0:RF, h % 2, :],
                                      u_hi[0:RF, q % USLOTS, h % QH, :].bitcast(F32), ALU.subtract)\
                       .then_inc(s["u_lo_done"], 1)

                add(0)
                for h in range(H):
                    if h + 1 < H:
                        add(h + 1)
                    low(h)
                root(b, "b", 1)
                wait("x2_hi_done", 1)
                eng.tensor_tensor(x2_lo, x2T, x2_hi.bitcast(F32), ALU.subtract).then_inc(s["x2_lo_done"], 1)
                for e in range(E):
                    if more and e == V_MEAN1:
                        root(b + 1, "f", 1)
                    if more and e == V_MEAN2:
                        root(b + 1, "f", 2)
                    wait("hid_hi_done", e + 1)
                    if e >= 3:
                        wait("moe_done", e - 2)
                    eng.tensor_tensor(hid_lo[e % 3], hid[:, e % 3, :], hid_hi[e % 3].bitcast(F32), ALU.subtract)\
                       .then_inc(s["hid_lo_done"], 1)

            root(0, "f", 1)
            root(0, "f", 2)
            with eng.Fori(0, B - 1) as b:
                batch(b, True)
            batch(B - 1, False)


_INS = ['L0_attn_hidden_states', 'L0_attn_Wq', 'L0_attn_bq', 'L0_attn_Wk', 'L0_attn_bk', 'L0_attn_Wv', 'L0_attn_bv',
        'L0_attn_Wo', 'L0_attn_bo', 'L0_ffn_wq', 'L0_ffn_wk', 'L0_ffn_wv', 'L0_ffn_wp', 'L0_ffn_wo', 'L0_ffn_ln1_g',
        'L0_ffn_ln1_b', 'L0_ffn_ln2_g', 'L0_ffn_ln2_b', 'L0_ffn_sel_w', 'L0_ffn_keys', 'L0_ffn_values']
_CONSTS = ["c_span", "c_cos", "c_sin", "c_key", "c_ident", "c_pick", "c_iota"]


def kernel(**inputs):
    import numpy as _np
    import concourse.bacc as _bacc
    from concourse import mybir as _mybir
    from concourse.bass_utils import run_bass_kernel_spmd as _run

    nc = _bacc.Bacc("TRN2", target_bir_lowering=False, num_devices=1)
    arrays, args = {}, []
    tables = position_constants()
    for name in _INS + _CONSTS:
        a = _np.ascontiguousarray(inputs[name] if name in inputs else tables[name])
        arrays[f"in_{name}_dram"] = a
        args.append(nc.dram_tensor(f"in_{name}_dram", a.shape, _mybir.dt.from_np(a.dtype), kind="ExternalInput").ap())
    args.append(nc.dram_tensor("out_0_dram", (B, S, P), F32, kind="ExternalOutput").ap())
    build(nc, *args)
    r = _run(nc, [arrays], core_ids=[0])
    return r.results[0]["out_0_dram"]
```

```python
from contextlib import ExitStack

import concourse.bass as bass
from concourse import mybir

F32 = mybir.dt.float32
FR = mybir.dt.float32r
U32 = mybir.dt.uint32
ALU = mybir.AluOpType
ACT = mybir.ActivationFunctionType
X = mybir.AxisListType.X

P = 128
B, S = 8, 512
T = S // P
H, HD = 16, 8
E, TOPK = 32, 4
NF = 59
RF = 2 * NF
RQ = RF + HD
RK = RQ + 1
QH = 4
NQ = H // QH
CE = S // P
NC = E // CE
USLOTS = 3
PSLOTS = 8
EPS = 1e-5
HEAD_SCALE = float(HD) ** -0.5
MAIN_SCALE = float(P) ** -0.5

SCORE_AT = 10
GUARD_AT = -13
TURN_AT = -20
NT = H * T
NT1 = QH * T
TICKS = SCORE_AT + NT + 10
MAIN_SCORE, MAIN_OUT = 0, 11

STATS1, MEAN1, NORM1, STATS2, MEAN2, NORM2, XN, Z, Y, VM, MG0, QK, MG1, V, MG2 = range(15)
FRONT_AT = {STATS1: 56, MEAN1: 57, NORM1: 58, STATS2: 59, MEAN2: 60, NORM2: 61, XN: 63, Z: 65, Y: 67, VM: 71}
MG3, MAIN_ROW = 1, 4
QUAD_AT = 5
PRE = 6
DENOM, INVERT = 1, (2, 15, 23, 31)
CUT = INVERT[-1] + 1
MULTIPLY, ADD = 13, 14
HCUT = ADD + 1
KEEP = 46
LAG = 3


def position_constants():
    import numpy as np

    freq = 1.0 / 10000.0 ** (np.arange(0, P, 2) / P)
    keep = 44
    n = NF - keep
    nodes2 = freq[keep] ** 2 * (1 + np.cos((2 * np.arange(n) + 1) * np.pi / (2 * n))) / 2
    nodes = np.sqrt(nodes2)
    low = freq[keep:]
    lag = np.array([[np.prod([(f * f - nodes2[m]) / (nodes2[k] - nodes2[m]) for m in range(n) if m != k])
                     for f in low] for k in range(n)])
    span = np.zeros((P, 2 * NF))
    for k in range(keep):
        span[k, k] = span[P // 2 + k, NF + k] = 1.0
    span[keep:P // 2, keep:NF] = (lag * low[None, :] / nodes[:, None]).T
    span[P // 2 + keep:, NF + keep:] = lag.T
    f = np.concatenate([freq[:keep], nodes])
    at = f[:, None] * np.arange(S)[None, :]
    sin, cos = np.sin(at), np.cos(at)
    swapped = np.concatenate([span[:, NF:], span[:, :NF]], axis=1)
    f32 = np.float32
    return {
        "c_span": np.concatenate([span, swapped], axis=1).astype(f32),
        "c_cos": np.concatenate([cos, cos]).astype(f32),
        "c_sin": np.concatenate([sin, -sin]).astype(f32),
        "c_key": np.concatenate([sin, cos]).astype(f32),
        "c_ident": np.eye(P, dtype=f32),
        "c_pick": np.concatenate([np.eye(E), np.eye(E)]).astype(f32),
        "c_iota": np.tile(np.arange(E, dtype=f32), (P, TOPK)),
    }


def build(nc, x, Wq, bq, Wk, bk, Wv, bv, Wo, bo, wq, wk, wv, wp, wo, ln1_g, ln1_b, ln2_g, ln2_b,
          sel_w, keys, values, c_span, c_cos, c_sin, c_key, c_ident, c_pick, c_iota, out):
    spill = nc.dram_tensor("spill", (4, P, S), F32, kind="Internal").ap()
    spill_w = nc.dram_tensor("spill_w", (2, P, 2 * RF), F32, kind="Internal").ap()
    low_keys = nc.dram_tensor("low_keys", (P, NC, S), F32, kind="Internal").ap()
    low_vals = nc.dram_tensor("low_vals", (P, NC, S), F32, kind="Internal").ap()
    spill_row = nc.dram_tensor("spill_row", (NQ, QH * T, P), F32, kind="Internal").ap()
    spill_main = nc.dram_tensor("spill_main", (T, P), F32, kind="Internal").ap()

    with ExitStack() as ctx:
        def sb(name, shape, dt=F32):
            return ctx.enter_context(nc.sbuf_tensor(name, shape, dt))

        def ps(name, shape, dt=F32):
            return ctx.enter_context(nc.psum_tensor(name, shape, dt))

        def sem(name):
            return ctx.enter_context(nc.semaphore(name))

        ident = sb("ident", [P, P])
        rot_a = sb("rot_a", [P, 2, S])
        rot_b = sb("rot_b", [P, 2, S])
        xres = sb("xres", [P, T, P])
        key_table = xres[0:RF, :, :].rearrange("p t d -> p (t d)")
        halves = [(rot_a, rot_b)[n // 4][:, n // 2 % 2, (n % 2) * 2 * P:(n % 2 + 1) * 2 * P] for n in range(6)]
        WqA, WkA, WvA, WoT = (v.rearrange("p (c n) -> p c n", c=2) for v in halves[0:4])
        WoA, span = halves[4], halves[5][:, 0:2 * RF]
        wpF, bo_row = rot_b[:, 1, 0:P], rot_b[:, 1, P:2 * P]
        prob = sb("prob", [P, PSLOTS, S])
        biasA = sb("biasA", [P, 3, 2])
        wqk = sb("wqk", [P, P])
        wvo = sb("wvo", [P, P + 1])
        y_bias = sb("y_bias", [P, 1])
        bqbk = sb("bqbk", [P, 1])
        out_bias = sb("out_bias", [P, P])
        wqF, wkF, wvF, woF = (sb(n, [P, P]) for n in ("wqF", "wkF", "wvF", "woF"))
        selF = sb("selF", [P, E])
        lnF = sb("lnF", [P, 4])
        keys_hi = sb("keys_hi", [P, E, P], FR)
        vals_hi = sb("vals_hi", [P, E, P], FR)
        cosT = sb("cosT", [RF, S])
        sinT = sb("sinT", [RF, S])
        pick = sb("pick", [2 * E, E], FR)
        iota = sb("iota", [P, TOPK, E])
        turn_w = sb("turn_w", [P, NQ, 2 * RF], FR)

        xin = sb("xin", [P, T, P])
        xn = sb("xn", [P, T, P])
        zn = sb("zn", [P, T, P])
        stats = sb("stats", [P, T, 6])
        mv = sb("mv", [P, T, 2])
        carrier = sb("carrier", [P, 1])
        rstd = sb("rstd", [P, T])
        var_eps = sb("var_eps", [P, T])
        eps = sb("eps", [P, T])
        minus_half = sb("minus_half", [P, T])
        xnT = sb("xnT", [P, S])
        xfT = sb("xfT", [P, S])
        yT = sb("yT", [P, S])
        vmain = sb("vmain", [P, T, P + 1])
        cmain = sb("cmain", [P, T])
        turn_q = sb("turn_q", [P, NQ, S], FR)
        vhead = sb("vhead", [P, T, H * (HD + 1) + 32])
        u_hi = sb("u_hi", [P, USLOTS, QH, S], FR)
        u_lo = sb("u_lo", [P, USLOTS, QH, S], FR)
        w_hi, w_lo = u_lo[:, 0, 0, 0:2 * RF], u_lo[:, 0, 1, 0:2 * RF]
        def keys_lo(e):
            return u_lo[:, 1, e // CE % QH, e % CE * P:(e % CE + 1) * P]

        def vals_lo(e):
            return u_lo[:, 2, e // CE % QH, e % CE * P:(e % CE + 1) * P]

        vals_low_stage = u_hi[:, 1:3, :, :].rearrange("p u g i -> p (u g) i")
        keys_low_stage = u_lo[:, 1:3, :, :].rearrange("p u g i -> p (u g) i")

        q_hi, q_lo, k_hi, k_lo = (prob[:, 3 + n, :].bitcast(FR) for n in range(4))
        k_hi4 = sb("k_hi4", [P, USLOTS, QH, S], FR)
        k_lo4 = sb("k_lo4", [P, USLOTS, QH, S], FR)
        rowmax = sb("rowmax", [P, 2, QH * T])
        rowmaxT = sb("rowmaxT", [QH * T, 2, P], FR)
        mmax = sb("mmax", [P, 3, T])
        mainrowT = sb("mainrowT", [T, P], FR)
        mainrow = u_hi[0:1, USLOTS - 1, 0, :]
        ones_row = sb("ones_row", [1, P], FR)
        smain = sb("smain", [P, T, P])
        rmain = sb("rmain", [P, T])
        oT = sb("oT", [P, S])
        rhead = sb("rhead", [P, T, QH])
        attn = sb("attn", [P, T, H, HD])
        attnT = oT
        src2 = sb("src2", [P, T, P])
        res = sb("res", [P, T, P])
        x2T = rot_a[:, 0, :]
        sel = sb("sel", [P, T, E])
        selx = sb("selx", [P, T, E])
        top = sb("top", [P, T, 8])
        topi = sb("topi", [P, T, 8], U32)
        topf = sb("topf", [P, T, 8])
        hit = attn[:, :, :, :].rearrange("p t h d -> p (t h d)").rearrange("p (t k e) -> p t k e", t=T, k=TOPK)
        gate = sb("gate", [P, T, E])
        pick32 = gate[0:2 * E, 0, :]
        gateT = sb("gateT", [2 * E, S], FR)
        hid = prob[:, 0:3, :]
        hid_hi = [u_hi[:, 1, n, :] for n in range(3)]
        hid_lo = [u_hi[:, 2, n, :] for n in range(3)]
        x2_hi, x2_lo = u_hi[:, 1, 3, :], u_hi[:, 2, 3, :]
        moeT = oT

        ps_turn = ps("ps_turn", [P, 2, S])
        ps_guard = ps("ps_guard", [P, 2, S])
        ps_score = ps("ps_score", [P, 2, S])
        ps_acc = ps("ps_acc", [P, 2, S])
        acc, mis = ps_acc[:, 0, :], ps_acc[:, 1, :]

        names = ("w_in x_in setup_pe setup_dve w_spilled w_turned dve_order xn_ready z_ready xnT_ps zT_ps xnT_ready "
                 "xfT_ready proj_ps proj_hi proj_done y_ready qk_spilled q_turned kq0 kq1 kq2 kq3 turn_ps rot_done "
                 "u_sum u_hi_done u_lo_done guard_ps max_done maxT_ps maxT_done row_out row_in score_ps exp_done pv_done "
                 "oT_done oTT_ps attn_done mg_ps mmax_done mmaxT_ps mmaxT_done mainrow_out mainrow_in main_done attnT_ps "
                 "attnT_ready wo_ps src2_ready z2T_ps vm_done x2T_ready x2_hi_done x2_lo_done hid_hi_done hid_lo_done keys_in vals_in0 vals_in1 vals_in2 vals_in3 weights_hi weights_lo vals_split k_tables low_spilled keys_lo_in3 keys_lo_in4 keys_lo_in5 keys_lo_in6 keys_lo_in7 vals_lo_in3 vals_lo_in4 vals_lo_in5 vals_lo_in6 vals_lo_in7 logit_ps logit_ready esel_done gate_ready gateT_ps gateT_hi gateT_done "
                 "hid_ps relu_done gsel_ps hg_done moe_done moeT_ready moeTT_ps fvar_ready fvar_eps frstd_ready bvar_ready bvar_eps brstd_ready final_ready silu_in esig_done batch_done stored half_set x_free scaled multiplied inverted xn_kept memset_done").split()
        s = {n: sem(n) for n in names}
        s_vals_in = [s[f"vals_in{i}"] for i in range(NC // 2)]
        s_kq = [s[f"kq{i}"] for i in range(NQ)]
        per = dict(x_in=16, xn_ready=1, z_ready=1, xnT_ps=1, zT_ps=1, xnT_ready=1, xfT_ready=1,
                   proj_ps=6, proj_hi=2, proj_done=3, y_ready=1, qk_spilled=64, q_turned=16 * 12, kq=64,
                   turn_ps=2 * H, rot_done=2 * H, u_sum=H, u_hi_done=H, u_lo_done=H, guard_ps=NT, max_done=NT,
                   maxT_ps=NQ, maxT_done=NQ, row_in=16 * NQ, row_out=16 * NQ, mainrow_out=16,
                   score_ps=NT + T, exp_done=NT + T, pv_done=NQ * T + T,
                   oT_done=NQ, oTT_ps=NQ, attn_done=NQ, mg_ps=T, mmax_done=T + 1, mmaxT_ps=1, mmaxT_done=1,
                   mainrow_in=16, main_done=1, attnT_ps=1, attnT_ready=1, wo_ps=1, src2_ready=1, z2T_ps=1,
                   x2T_ready=1, x2_hi_done=1, x2_lo_done=1, hid_hi_done=E, hid_lo_done=E, lo_in=16,
                   logit_ps=1, logit_ready=1, esel_done=1, gate_ready=1, gateT_ps=1, gateT_hi=1, gateT_done=1,
                   hid_ps=E, relu_done=E, gsel_ps=E, hg_done=E, moe_done=E, moeT_ready=1, moeTT_ps=1,
                   final_ready=1, fvar_ready=2, fvar_eps=2, frstd_ready=2, bvar_ready=1, bvar_eps=1, brstd_ready=1,
                   vm_done=2, silu_in=1, esig_done=1, batch_done=1, stored=16, x_free=1, inverted=T, scaled=1, multiplied=1, xn_kept=1)
        FLINK, NLINK = 3 + (MAIN_OUT < CUT), 18
        NW = 28 * 16

        block = ctx.enter_context(nc.Block())

        def main_slot(jb):
            return jb

        def guard_bank(n, alone=False):
            return 1 if n < NT1 and not alone else n % 2

        mg_bank = (ps_guard[:, 0, :], ps_guard[:, 1, :], ps_turn[:, 1, :], ps_turn[:, 0, :])

        def bank_of(n):
            return n % 2

        def pslot(n):
            return (n + T) % PSLOTS

        @block.sync
        def _(eng):
            def load(dst, src):
                eng.dma_start(dst, src).then_inc(s["w_in"], 16)

            eng.dma_start(xin[:, :, :], x[0].rearrange("(t p) d -> p t d", p=P)).then_inc(s["x_in"], 16)
            for dst, src in ((WqA, Wq), (WkA, Wk), (WvA, Wv)):
                load(dst[:, :, :], src.rearrange("(c p) d -> p c d", p=P))
            load(WoA, Wo)
            load(ident[:, :], c_ident)
            for n, src in enumerate((bq, bk, bv)):
                for c in range(2):
                    load(biasA[:, n, c:c + 1], src.rearrange("(c p o) -> c p o", c=2, o=1)[c])
            load(bo_row, bo.partition_broadcast(P))
            for dst, src in ((wqF, wq), (wkF, wk), (wvF, wv), (woF, wo), (selF, sel_w)):
                load(dst[:, :], src)
            for n, src in enumerate((ln1_g, ln1_b, ln2_g, ln2_b)):
                load(lnF[:, n:n + 1], src.rearrange("(p o) -> p o", o=1))
            load(wpF, wp)
            load(span, c_span)
            load(cosT[:, :], c_cos)
            load(sinT[:, :], c_sin)
            load(key_table, c_key)
            load(pick32, c_pick)
            load(iota[:, :, :], c_iota.rearrange("p (k e) -> p k e", k=TOPK))
            eng.dma_start(prob[:, :, :].rearrange("p c (e h) -> p (c e) h", h=P), keys.rearrange("e d h -> d e h"))\
                .then_inc(s["keys_in"], 16)

            eng.wait_ge(s["setup_dve"], 6)
            eng.dma_start(spill_w[0], w_hi.bitcast(F32)).then_inc(s["w_spilled"], 16)
            eng.dma_start(spill_w[1], w_lo.bitcast(F32)).then_inc(s["w_spilled"], 16)
            eng.wait_ge(s["w_spilled"], 32)
            for g in range(QH):
                for r, part in enumerate((0, 0, 1)):
                    src = spill_w[part].rearrange("(q g d) n -> g d q n", g=QH, d=HD)[g]
                    eng.dma_start(turn_w[32 * g + HD * r:32 * g + HD * (r + 1), :, :].bitcast(F32), src)\
                       .then_inc(s["w_turned"], 16)

            def low_weights(b):
                for c in range(QH, NC):
                    for done, dst, src, name in (("hid_ps", 1, low_keys, "keys_lo_in"),
                                                 ("moe_done", 2, low_vals, "vals_lo_in")):
                        eng.wait_ge(s[done], b * per[done] + CE * (c - QH + 1))
                        eng.dma_start(u_lo[:, dst, c % QH, :].bitcast(F32), src[:, c, :])\
                            .then_inc(s[f"{name}{c}"], 16)

            def quad_rows(q, parts):
                for dst, part in parts:
                    src = spill[part].rearrange("(q g d) i -> q d g i", g=QH, d=HD)[q]
                    eng.dma_start(dst[RF:RQ, q % USLOTS, :, :].bitcast(F32), src).then_inc(s_kq[q], 16)

            def guard_row(b, q):
                def wait(name, k):
                    eng.wait_ge(s[name], b * per[name] + k)

                wait("maxT_done", q + 1)
                eng.dma_start(spill_row[q], rowmaxT[:, q % 2, :].bitcast(F32)).then_inc(s["row_out"], 16)
                wait("row_out", 16 * (q + 1))
                eng.dma_start(u_hi[RQ:RK, q % USLOTS, :, :].bitcast(F32),
                              spill_row[q].rearrange("(o g t) i -> o g (t i)", o=1, g=QH)).then_inc(s["row_in"], 16)

            def front(b, beside):
                def wait(name, k):
                    eng.wait_ge(s[name], b * per[name] + k)

                wait("proj_done", 2)
                for n, src in enumerate((q_hi, q_lo, k_hi, k_lo)):
                    eng.dma_start(spill[n], src.bitcast(F32)).then_inc(s["qk_spilled"], 16)
                wait("qk_spilled", 64)
                for g in range(QH):
                    for r, part in enumerate((0, 1, 0)):
                        src = spill[part].rearrange("(q g d) i -> g d q i", g=QH, d=HD)[g]
                        eng.dma_start(turn_q[32 * g + HD * r:32 * g + HD * (r + 1), :, :].bitcast(F32), src)\
                           .then_inc(s["q_turned"], 16)
                quad_rows(0, ((u_hi, 0), (u_lo, 1), (k_hi4, 2), (k_lo4, 3)))
                for q in range(1, USLOTS):
                    quad_rows(q, ((k_hi4, 2), (k_lo4, 3)))
                if beside:
                    low_weights(b - 1)
                else:
                    eng.wait_ge(s["weights_lo"], NC)
                    eng.dma_start(low_keys, keys_low_stage.bitcast(F32)).then_inc(s["low_spilled"], 16)
                    eng.wait_ge(s["vals_split"], NC)
                    eng.dma_start(low_vals, vals_low_stage.bitcast(F32)).then_inc(s["low_spilled"], 16)
                    eng.wait_ge(s["low_spilled"], 32)
                wait("mmaxT_done", 1)
                eng.dma_start(spill_main, mainrowT[:, :].bitcast(F32)).then_inc(s["mainrow_out"], 16)
                if beside:
                    eng.wait_ge(s["moe_done"], b * per["moe_done"])
                wait("mainrow_out", 16)
                eng.dma_start(mainrow.bitcast(F32), spill_main.rearrange("(o t) i -> o (t i)", o=1))\
                    .then_inc(s["mainrow_in"], 16)
                for q in range(1, USLOTS):
                    quad_rows(q, ((u_hi, 0), (u_lo, 1)))
                guard_row(b, 0)

            def early(b):
                def wait(name, k):
                    eng.wait_ge(s[name], b * per[name] + k)

                guard_row(b, 1)
                wait("score_ps", T + NT1)
                quad_rows(NQ - 1, ((u_hi, 0), (u_lo, 1), (k_hi4, 2), (k_lo4, 3)))
                guard_row(b, 2)
                wait("score_ps", T + 2 * NT1)
                eng.dma_start(u_lo[:, 1, :, :].bitcast(F32), low_keys[:, 0:QH, :])\
                    .then_inc(s[f"keys_lo_in{QH - 1}"], 16)

            def batch(b, more):
                def wait(name, k):
                    eng.wait_ge(s[name], b * per[name] + k)

                if more:
                    wait("x_free", 1)
                    load_x(b + 1)
                guard_row(b, 3)
                wait("score_ps", T + 3 * NT1)
                eng.dma_start(u_lo[:, 2, :, :].bitcast(F32), low_vals[:, 0:QH, :])\
                    .then_inc(s[f"vals_lo_in{QH - 1}"], 16)
                if more:
                    front(b + 1, True)
                    early(b + 1)
                else:
                    low_weights(b)
                wait("batch_done", 2)
                eng.dma_start(out[b].rearrange("(t p) d -> p t d", p=P), res[:, :, :]).then_inc(s["stored"], 16)

            def load_x(b):
                eng.dma_start(xin[:, :, :], x[b].rearrange("(t p) d -> p t d", p=P)).then_inc(s["x_in"], 16)

            for c in range(0, NC, 2):
                eng.wait_ge(s["weights_lo"], c + 2)
                eng.dma_start(prob[:, c:c + 2, :].rearrange("p c (e h) -> p (c e) h", h=P),
                              values[CE * c:CE * c + 2 * CE].rearrange("e h d -> h e d"))\
                    .then_inc(s_vals_in[c // 2], 16)
            front(0, False)
            early(0)
            with eng.Fori(0, B - 1) as b:
                batch(b, True)
            batch(B - 1, False)
            eng.wait_ge(s["stored"], 16 * (B + 1))

        @block.tensor
        def _(eng):
            mm, tr = eng.matmul, eng.transpose
            eng.wait_ge(s["w_in"], NW)
            for c in range(2):
                tr(ps_turn[:, 0, c * P:(c + 1) * P], WoA[:, c * P:(c + 1) * P], ident[:, :])
            tail = mm(ps_turn[:, 1, 0:2 * RF], wpF, span, start=True, stop=True)
            tail.then_inc(s["setup_pe"], 1)
            eng.wait_ge(s["setup_dve"], 1)
            for c in range(2):
                mm(ps_score[:, 0, 0:P], WqA[:, c, :], WkA[:, c, :], start=c == 0, stop=c == 1)
            for c in range(2):
                mm(ps_score[:, 1, 0:P], WvA[:, c, :], WoT[:, c, :], start=c == 0, stop=c == 1)
            for c in range(2):
                mm(ps_guard[:, 0, 0:1], WkA[:, c, :], biasA[:, 0, c:c + 1], start=c == 0, stop=c == 1)
            for c in range(2):
                mm(ps_guard[:, 1, 0:1], WqA[:, c, :], biasA[:, 1, c:c + 1], start=c == 0, stop=c == 1)
            for c in range(2):
                mm(mis[:, 0:1], biasA[:, 0, c:c + 1].to_broadcast([P, P]), biasA[:, 1, c:c + 1],
                   start=c == 0, stop=c == 1)
            for c in range(2):
                tail = mm(acc[:, 0:P], biasA[:, 2, c:c + 1].to_broadcast([P, P]), WoT[:, c, :],
                          start=c == 0, stop=c == 1)
            tail.then_inc(s["setup_pe"], 1)
            eng.wait_ge(s["setup_dve"], 12)

            def front(b, at):
                def wait(name, k):
                    eng.wait_ge(s[name], b * per[name] + k)

                if at == XN:
                    wait("xn_ready", 1)
                    for t in range(T):
                        tail = tr(ps_turn[:, 0, t * P:(t + 1) * P], xn[:, t, :], ident[:, :])
                    tail.then_inc(s["xnT_ps"], 1)
                if at == Z:
                    wait("z_ready", 1)
                    for t in range(T):
                        tail = tr(ps_turn[:, 1, t * P:(t + 1) * P], zn[:, t, :], ident[:, :])
                    tail.then_inc(s["zT_ps"], 1)
                if at == Y:
                    wait("xnT_ready", 1)
                    mm(ps_turn[:, 0, :], wqk[:, :], xnT[:, :], start=True, stop=True).then_inc(s["proj_ps"], 1)
                    wait("xfT_ready", 1)
                    values_main(b, 0)
                if at == VM:
                    wait("y_ready", 1)
                    values_main(b, 1)
                if at == QK:
                    wait("vm_done", 2)
                    mm(ps_turn[:, 0, :], wqF[:, :], xfT[:, :], start=True, stop=True).then_inc(s["proj_ps"], 1)
                    mm(ps_turn[:, 1, :], wkF[:, :], xfT[:, :], start=True, stop=True).then_inc(s["proj_ps"], 1)
                if at == V:
                    wait("proj_done", 1)
                    for t in range(T):
                        tail = mm(ps_turn[:, 0, t * P:(t + 1) * P], xfT[:, t * P:(t + 1) * P], wvF[:, :],
                                  start=t == 0, stop=t == T - 1, skip_group_check=True)
                    tail.then_inc(s["proj_ps"], 1)
                if at == MG0:
                    main_guard(b, 0)
                if at == MG1:
                    main_guard(b, 1)
                if at == MG2:
                    wait("proj_done", 2)
                    main_guard(b, 2)

            def main_guard(b, m):
                mm(mg_bank[m], yT[:, m * P:(m + 1) * P], xnT[:, :], start=True, stop=True).then_inc(s["mg_ps"], 1)

            def values_main(b, c):
                for t in range(2 * c, 2 * c + 2):
                    tail = mm(ps_turn[:, 1 - c, (t % 2) * (P + 1):(t % 2 + 1) * (P + 1)],
                              xnT[:, t * P:(t + 1) * P], wvo[:, :], start=t % 2 == 0, stop=t % 2 == 1,
                              skip_group_check=True)
                tail.then_inc(s["proj_ps"], 1)

            def turn(b, h):
                def wait(name, k):
                    eng.wait_ge(s[name], b * per[name] + k)

                g = h % QH
                if h == 0:
                    wait("q_turned", 12 * 16)
                    wait("mmax_done", T)
                if h >= 1:
                    wait("rot_done", 2 * h - 1)
                rows = slice(32 * g, 32 * g + 3 * HD)
                mm(ps_turn[0:RF, 0, :], turn_w[rows, h // QH, 0:RF], turn_q[rows, h // QH, :],
                   start=True, stop=True).then_inc(s["turn_ps"], 1)
                if h >= 1:
                    wait("rot_done", 2 * h)
                mm(ps_turn[0:RF, 1, :], turn_w[rows, h // QH, RF:2 * RF], turn_q[rows, h // QH, :],
                   start=True, stop=True).then_inc(s["turn_ps"], 1)

            def guard(b, n, alone=False):
                def wait(name, k):
                    eng.wait_ge(s[name], b * per[name] + k)

                h, ib = n // T, n % T
                q, g = h // QH, h % QH
                if ib == 0:
                    wait("u_hi_done", h + 1)
                if n % NT1 == 0:
                    eng.wait_ge(s_kq[q], b * per["kq"] + 64)
                bank = guard_bank(n, alone)
                if n >= 1 and bank == guard_bank(n - 1, alone):
                    wait("max_done", n)
                elif n >= 2:
                    wait("max_done", n - 1)
                mm(ps_guard[:, bank, :], u_hi[0:RQ, q % USLOTS, g, ib * P:(ib + 1) * P],
                   k_hi4[0:RQ, q % USLOTS, g, :], start=True, stop=True).then_inc(s["guard_ps"], 1)

            def row_max(b, q):
                def wait(name, k):
                    eng.wait_ge(s[name], b * per[name] + k)

                wait("max_done", NT1 * (q + 1))
                if q == 0:
                    wait("mmaxT_done", 1)
                else:
                    wait("maxT_done", q)
                if q == 1:
                    wait("main_done", 1)
                if q >= 2:
                    wait("attn_done", q - 1)
                tr(mis[0:QH * T, 0:P], rowmax[:, q % 2, :], ident[:, :]).then_inc(s["maxT_ps"], 1)

            def beside(b, e, alone=False):
                def wait(name, k):
                    eng.wait_ge(s[name], b * per[name] + k)

                if e == MG3:
                    wait("proj_done", 3)
                    main_guard(b, 3)
                if e == MAIN_ROW:
                    wait("mmax_done", T + 1)
                    tr(mis[0:T, 0:P], mmax[:, 2, :], ident[:, :]).then_inc(s["mmaxT_ps"], 1)
                p = e - QUAD_AT
                if p >= 0 and p % 4 == 0 and p // 4 < PRE:
                    turn(b, p // 4)
                if 0 <= p - 6 < NT1:
                    guard(b, p - 6, alone)
                if p - 6 == NT1:
                    row_max(b, 0)

            def batch(b, more):
                def wait(name, k):
                    eng.wait_ge(s[name], b * per[name] + k)

                for tick in range(TICKS):
                    if more and tick == FRONT_AT[XN]:
                        wait("rot_done", 2 * H)
                        front(b + 1, XN)
                    for at in (Z, Y, VM):
                        if more and tick == FRONT_AT[at]:
                            front(b + 1, at)
                    m = (tick - MAIN_SCORE)
                    if 0 <= m < 2 * T and m % 2 == 0:
                        jb = m // 2
                        if jb >= 2:
                            wait("exp_done", jb - 1)
                        mm(ps_score[:, jb % 2, :], xnT[:, jb * P:(jb + 1) * P], yT[:, :], start=True, stop=False)
                        if jb == 0:
                            wait("mainrow_in", 16)
                        mm(ps_score[:, jb % 2, :], ones_row[:, :], mainrow, start=False, stop=True)\
                            .then_inc(s["score_ps"], 1)
                    if 2 <= m < 2 * T + 2 and m % 2 == 0:
                        jb = m // 2 - 1
                        wait("exp_done", jb + 1)
                        if jb == 0:
                            wait("final_ready", 1)
                        for ib in range(T):
                            tail = mm(ps_acc[:, ib // 2, (ib % 2) * (P + 1):(ib % 2 + 1) * (P + 1)],
                                      prob[:, main_slot(jb), ib * P:(ib + 1) * P], vmain[:, jb, :],
                                      start=jb == 0 and ib % 2 == 0, stop=jb == T - 1 and ib % 2 == 1,
                                      skip_group_check=True)
                        tail.then_inc(s["pv_done"], 1)

                    if (tick - TURN_AT) % 4 == 0 and PRE <= (tick - TURN_AT) // 4 < H:
                        turn(b, (tick - TURN_AT) // 4)
                    n = tick - SCORE_AT
                    if 0 <= n < NT:
                        q, jb, g = n // 16, n // 4 % 4, n % 4
                        slot = q % USLOTS
                        if n % 16 == 0:
                            wait("u_lo_done", QH * (q + 1))
                            wait("row_in", 16 * (q + 1))
                        wait("exp_done", T + n - 1)
                        ko = slice(jb * P, (jb + 1) * P)
                        o = ps_score[:, bank_of(n), :]
                        mm(o, k_hi4[0:RK, slot, g, ko], u_hi[0:RK, slot, g, :], start=True, stop=False)
                        mm(o, k_hi4[0:RQ, slot, g, ko], u_lo[0:RQ, slot, g, :], start=False, stop=False)
                        mm(o, k_lo4[0:RK, slot, g, ko], u_hi[0:RK, slot, g, :], start=False, stop=True)\
                            .then_inc(s["score_ps"], 1)
                    n = tick - GUARD_AT
                    if NT1 <= n < NT:
                        guard(b, n)
                    if n % NT1 == 0 and 1 < n // NT1 <= NQ:
                        row_max(b, n // NT1 - 1)
                    n = tick - SCORE_AT - 6
                    if n >= 0 and n % 4 == 0 and n // 4 < NQ * T:
                        m = n // 4
                        q, jb = m // T, m % T
                        wait("exp_done", T + 4 * (m + 1))
                        if jb == 0:
                            if q == 0:
                                wait("main_done", 1)
                            else:
                                wait("oT_done", q)
                        for g in range(QH):
                            c = (QH * q + g) * (HD + 1)
                            tail = mm(acc[32 * g:32 * g + 32, :], vhead[:, jb, c:c + 32],
                                      prob[:, pslot(4 * m + g), :], start=jb == 0, stop=jb == T - 1)
                        tail.then_inc(s["pv_done"], 1)
                    n = tick - SCORE_AT - 21
                    if n >= 0 and n % 16 == 0 and n // 16 < NQ:
                        q = n // 16
                        wait("oT_done", q + 1)
                        wait("maxT_done", min(q + 2, NQ))
                        if q >= 1:
                            wait("attn_done", q)
                        for t in range(T):
                            tail = tr(mis[:, t * P:(t + 1) * P], oT[:, t * P:(t + 1) * P], ident[:, :])
                        tail.then_inc(s["oTT_ps"], 1)

                wait("attn_done", NQ)
                for t in range(T):
                    tail = tr(mis[:, t * P:(t + 1) * P], attn[:, t, :, :].rearrange("p h d -> p (h d)"), ident[:, :])
                tail.then_inc(s["attnT_ps"], 1)
                if more:
                    wait("max_done", NT)
                    front(b + 1, MG0)
                wait("attnT_ready", 1)
                for t in range(T):
                    tail = mm(acc[:, t * P:(t + 1) * P], attnT[:, t * P:(t + 1) * P], woF[:, :],
                              start=t == 0, stop=t == T - 1, skip_group_check=True)
                tail.then_inc(s["wo_ps"], 1)
                if more:
                    front(b + 1, QK)
                    front(b + 1, MG1)
                wait("src2_ready", 1)
                for t in range(T):
                    tail = tr(mis[:, t * P:(t + 1) * P], zn[:, t, :], ident[:, :])
                tail.then_inc(s["z2T_ps"], 1)
                wait("x2T_ready", 1)
                for t in range(T):
                    tail = mm(acc[:, t * E:(t + 1) * E], x2T[:, t * P:(t + 1) * P], selF[:, :],
                              start=t == 0, stop=t == T - 1, skip_group_check=True)
                tail.then_inc(s["logit_ps"], 1)

                def hidden(e):
                    if e >= 2:
                        wait("relu_done", e - 1)
                    if e % CE == 0 and (e == 0 or e >= QH * CE):
                        eng.wait_ge(s[f"keys_lo_in{max(e // CE, QH - 1)}"], b * per["lo_in"] + 16)
                    o = ps_score[:, e % 2, :]
                    mm(o, keys_hi[:, e, :], x2_hi, start=True, stop=False)
                    mm(o, keys_lo(e), x2_hi, start=False, stop=False)
                    if e == 0:
                        wait("x2_lo_done", 1)
                    mm(o, keys_hi[:, e, :], x2_lo, start=False, stop=True).then_inc(s["hid_ps"], 1)

                def gate_row(e):
                    if e >= 1:
                        wait("hg_done", e)
                    mm(ps_guard[:, 0, :], pick[:, e:e + 1].to_broadcast([2 * E, P]), gateT[:, :],
                       start=True, stop=True).then_inc(s["gsel_ps"], 1)

                if more:
                    front(b + 1, V)
                wait("x2_hi_done", 1)
                hidden(0)
                hidden(1)
                if more:
                    front(b + 1, MG2)
                wait("gate_ready", 1)
                for t in range(T):
                    tail = tr(mis[0:E, t * P:(t + 1) * P], gate[:, t, :], ident[:, :])
                tail.then_inc(s["gateT_ps"], 1)
                wait("gateT_done", 1)
                if more:
                    eng.wait_ge(s["mmax_done"], (b + 1) * per["mmax_done"] + 1)
                for e in range(E + LAG):
                    if more and e < E:
                        beside(b + 1, e)
                    if 2 <= e < E:
                        hidden(e)
                    if e < LAG:
                        gate_row(e)
                    if e >= LAG:
                        f = e - LAG
                        if f % CE == 0 and (f == 0 or f >= QH * CE):
                            eng.wait_ge(s[f"vals_lo_in{max(f // CE, QH - 1)}"], b * per["lo_in"] + 16)
                        wait("hid_hi_done", f + 1)
                        if f == 0:
                            wait("logit_ready", 1)
                        mm(acc, vals_hi[:, f, :], hid_hi[f % 3], start=f == 0, stop=False)
                        mm(acc, vals_lo(f), hid_hi[f % 3], start=False, stop=False)
                        wait("hid_lo_done", f + 1)
                        mm(acc, vals_hi[:, f, :], hid_lo[f % 3], start=False, stop=f == E - 1)\
                            .then_inc(s["moe_done"], 1)
                        if e < E:
                            gate_row(e)
                if more:
                    eng.wait_ge(s["maxT_done"], (b + 1) * per["maxT_done"] + 1)
                wait("moeT_ready", 1)
                for t in range(T):
                    tail = tr(mis[:, t * P:(t + 1) * P], moeT[:, t * P:(t + 1) * P], ident[:, :])
                tail.then_inc(s["moeTT_ps"], 1)

            for at in range(MG2 + 1):
                front(0, at)
            eng.wait_ge(s["w_turned"], 12 * 16)
            for e in range(E):
                beside(0, e, alone=True)
            eng.wait_ge(s["k_tables"], 1)
            with eng.Fori(0, B - 1) as b:
                batch(b, True)
            batch(B - 1, False)

        @block.vector
        def _(eng):
            def setup(ins):
                ins.then_inc(s["setup_dve"], 1)

            eng.memset(vhead[:, :, :], 1.0).then_inc(s["memset_done"], 1)
            eng.memset(vmain[:, :, :], 1.0).then_inc(s["memset_done"], 1)
            eng.memset(ones_row[:, :].bitcast(F32), 1.0).then_inc(s["memset_done"], 1)
            links, chain = [0], [0]

            def link(ins, fixed=False):
                links[0] += 1
                ins.then_inc(s["dve_order"], 1)
                eng.wait_ge(s["dve_order"], chain[0] + links[0])
                if fixed:
                    eng.memset(carrier[:, :], 0.0)

            def norm_stats(src):
                for t in range(T):
                    i = eng.bn_stats(stats[:, t, :], src[:, t, :])
                link(i, fixed=True)

            def norm_mean(ready):
                for t in range(T):
                    i = eng.bn_aggr(mv[:, t, :], stats[:, t, :])
                i.then_inc(s[ready], 1)

            def norm_apply(dst, src, done):
                for t in range(T):
                    i = eng.tensor_scalar(dst[:, t, :], src[:, t, :], mv[:, t, 0:1], rstd[:, t:t + 1],
                                        ALU.subtract, ALU.mult)
                i.then_inc(s[done], 1)

            def front(b, at):
                def wait(name, k):
                    eng.wait_ge(s[name], b * per[name] + k)

                if at == STATS1:
                    wait("x_in", 16)
                    norm_stats(xin)
                if at == MEAN1:
                    norm_mean("fvar_ready")
                if at == NORM1:
                    wait("frstd_ready", 1)
                    norm_apply(xn, xin, "xn_ready")
                if at == STATS2:
                    wait("xn_ready", 1)
                    eng.memset(carrier[:, :], 0.0)
                    norm_stats(xn)
                if at == MEAN2:
                    norm_mean("fvar_ready")
                if at == NORM2:
                    wait("frstd_ready", 2)
                    norm_apply(zn, xn, "z_ready")
                if at == Z:
                    wait("zT_ps", 1)
                    eng.tensor_scalar(xfT[:, :], ps_turn[:, 1, :], lnF[:, 0:1], lnF[:, 1:2], ALU.mult, ALU.add)\
                        .then_inc(s["xfT_ready"], 1)
                if at == QK:
                    for n, (lo, hi) in enumerate(((q_lo, q_hi), (k_lo, k_hi))):
                        wait("proj_hi", n + 1)
                        eng.tensor_tensor(lo, ps_turn[:, n, :], hi.bitcast(F32), ALU.subtract)\
                            .then_inc(s["proj_done"], 1)
                if at == Y:
                    values_main(b, 0)
                if at == VM:
                    values_main(b, 1)
                if at == V:
                    wait("proj_ps", 6)
                    eng.tensor_copy(vhead[:, :, 0:H * (HD + 1)].rearrange("p t (h c) -> p t h c", h=H)[:, :, :, 0:HD],
                                    ps_turn[:, 0, :].rearrange("p (t h c) -> p t h c", t=T, h=H))\
                        .then_inc(s["proj_done"], 1)
                if at in (MG0, MG1, MG2):
                    main_max(b, (MG0, MG1, MG2).index(at))

            def values_main(b, c):
                eng.wait_ge(s["proj_ps"], b * per["proj_ps"] + 2 + c)
                pv = ps_turn[:, 1 - c, 0:2 * (P + 1)].rearrange("p (t n) -> p t n", t=2)
                eng.tensor_copy(vmain[:, 2 * c:2 * c + 2, 0:P], pv[:, :, 0:P])
                eng.tensor_scalar(cmain[:, 2 * c:2 * c + 2], pv[:, :, P], bqbk[:, 0:1], None, ALU.add)\
                    .then_inc(s["vm_done"], 1)

            def main_max(b, m):
                eng.wait_ge(s["mg_ps"], b * per["mg_ps"] + m + 1)
                eng.tensor_reduce(mmax[:, 0, m:m + 1], mg_bank[m], X, ALU.max).then_inc(s["mmax_done"], 1)

            def turn(b, h, n):
                def wait(name, k):
                    eng.wait_ge(s[name], b * per[name] + k)

                if h >= 2 and n == 0:
                    wait("u_lo_done", h - 1)
                wait("turn_ps", 2 * h + n + 1)
                rot, table = ((rot_a, cosT), (rot_b, sinT))[n]
                eng.tensor_tensor(rot[0:RF, h % 2, :], ps_turn[0:RF, n, :], table[:, :], ALU.mult)\
                    .then_inc(s["rot_done"], 1)

            def guard(b, n, alone=False):
                def wait(name, k):
                    eng.wait_ge(s[name], b * per[name] + k)

                q = n // NT1
                if n % NT1 == 0 and q >= 2:
                    wait("maxT_ps", q - 1)
                wait("guard_ps", n + 1)
                eng.tensor_reduce(rowmax[:, q % 2, n % NT1:n % NT1 + 1], ps_guard[:, guard_bank(n, alone), :], X, ALU.max)\
                    .then_inc(s["max_done"], 1)

            def beside(b, e, alone=False):
                def wait(name, k):
                    eng.wait_ge(s[name], b * per[name] + k)

                if e == MG3 + 1:
                    main_max(b, 3)
                    wait("mmax_done", T)
                    wait("vm_done", 2)
                    link(eng.tensor_tensor(mmax[:, 1, :], mmax[:, 0, :], cmain[:, :], ALU.add))
                    eng.tensor_tensor(mmax[:, 2, :], cmain[:, :], mmax[:, 1, :], ALU.subtract)\
                        .then_inc(s["mmax_done"], 1)
                p = e - QUAD_AT
                if p >= 0 and p % 4 < 2 and p // 4 < PRE:
                    turn(b, p // 4, p % 4)
                if 0 <= p - 6 < NT1:
                    guard(b, p - 6, alone)

            def step(b, tick, more):
                def wait(name, k):
                    eng.wait_ge(s[name], b * per[name] + k)

                for at in (STATS1, MEAN1, NORM1, STATS2, MEAN2, NORM2, Z, Y, VM):
                    if more and tick == FRONT_AT[at] + (at > NORM2):
                        if at == NORM1:
                            wait("xn_kept", 1)
                        front(b + 1, at)
                if tick == MAIN_OUT:
                    wait("pv_done", T)
                    wait("scaled", 1)
                    for c in range(2):
                        pa = ps_acc[:, c, 0:2 * (P + 1)].rearrange("p (t n) -> p t n", t=2)
                        i = eng.reciprocal(rmain[:, 2 * c:2 * c + 2], pa[:, :, P])
                    link(i)
                    for t in range(T):
                        o = (t % 2) * (P + 1)
                        i = eng.scalar_tensor_tensor(smain[:, t, :], ps_acc[:, t // 2, o:o + P], rmain[:, t:t + 1],
                                                     out_bias[:, :], ALU.mult, ALU.add)
                    i.then_inc(s["main_done"], 1)
                n = tick - GUARD_AT
                if NT1 <= n < NT:
                    guard(b, n)
                if (tick - TURN_AT) % 4 == 0 and PRE <= (tick - TURN_AT) // 4 < H:
                    for n in range(2):
                        turn(b, (tick - TURN_AT) // 4, n)
                n = tick - SCORE_AT - 22
                if n >= 0 and n % 16 == 0 and n // 16 < NQ:
                    q = n // 16
                    wait("oTT_ps", q + 1)
                    pt = mis.rearrange("p (t g r) -> p t g r", t=T, g=QH)
                    link(eng.reciprocal(rhead[:, :, :], pt[:, :, :, HD]))
                    eng.tensor_tensor(attn[:, :, QH * q:QH * q + QH, :], pt[:, :, :, 0:HD],
                                      rhead[:, :, :].unsqueeze(3).to_broadcast([P, T, QH, HD]), ALU.mult)\
                        .then_inc(s["attn_done"], 1)

            def finish(b, tick):
                def wait(name, k):
                    eng.wait_ge(s[name], b * per[name] + k)

                if tick == DENOM:
                    wait("esig_done", 1)
                    wait("stored", 16)
                    link(eng.tensor_scalar(res[:, :, :], oT[:, :].rearrange("p (t d) -> p t d", t=T), 1.0, None,
                                           ALU.add))
                if tick in INVERT:
                    t = INVERT.index(tick)
                    eng.reciprocal(res[:, t, :], res[:, t, :]).then_inc(s["inverted"], 1)

            def batch(b, more):
                def wait(name, k):
                    eng.wait_ge(s[name], b * per[name] + k)

                links[0], chain[0] = 0, b * NLINK + FLINK
                for tick in range(CUT, TICKS):
                    step(b, tick, more)

                wait("xn_kept", 1)
                wait("wo_ps", 1)
                link(eng.tensor_tensor(src2[:, :, :], acc.rearrange("p (t d) -> p t d", t=T), src2[:, :, :], ALU.add))
                norm_stats(src2)
                norm_mean("bvar_ready")
                wait("brstd_ready", 1)
                norm_apply(zn, src2, "src2_ready")
                wait("z2T_ps", 1)
                eng.tensor_scalar(x2T, mis, lnF[:, 2:3], lnF[:, 3:4], ALU.mult, ALU.add)\
                    .then_inc(s["x2T_ready"], 1)
                if more:
                    front(b + 1, QK)
                wait("logit_ps", 1)
                eng.tensor_scalar(selx[:, :, :], acc[:, 0:T * E].rearrange("p (t e) -> p t e", t=T), -87.0, None,
                                ALU.max).then_inc(s["logit_ready"], 1)
                if more:
                    front(b + 1, MG0)
                    front(b + 1, MG1)
                wait("esel_done", 1)
                link(eng.tensor_scalar(selx[:, :, :], sel[:, :, :], 1.0, None, ALU.add))
                link(eng.reciprocal(sel[:, :, :], selx[:, :, :]), fixed=True)
                for t in range(T):
                    i = eng.max(top[:, t, :], sel[:, t, :])
                link(i, fixed=True)
                for t in range(T):
                    i = eng.max_index(topi[:, t, :], top[:, t, :], sel[:, t, :])
                link(i)
                link(eng.tensor_copy(topf[:, :, :], topi[:, :, :]))
                for t in range(T):
                    i = eng.tensor_tensor(hit[:, t, :, :], iota[:, :, :],
                                        topf[:, t, 0:TOPK].unsqueeze(2).to_broadcast([P, TOPK, E]), ALU.is_equal)
                link(i)
                link(eng.tensor_reduce(selx[:, :, :], hit[:, :, :, :].rearrange("p t k e -> p t e k"), X, ALU.add))
                eng.tensor_tensor(gate[:, :, :], sel[:, :, :], selx[:, :, :], ALU.mult).then_inc(s["gate_ready"], 1)
                wait("gateT_hi", 1)
                eng.tensor_tensor(gateT[E:2 * E, :], mis[0:E, :], gateT[0:E, :].bitcast(F32), ALU.subtract)\
                    .then_inc(s["gateT_done"], 1)

                for e in range(E):
                    if more and e == 0:
                        front(b + 1, V)
                        front(b + 1, MG2)
                    if more:
                        beside(b + 1, e)
                    wait("relu_done", e + 1)
                    wait("gsel_ps", e + 1)
                    eng.tensor_tensor(hid[:, e % 3, :], ps_guard[:, 0, :], hid[:, e % 3, :], ALU.mult)\
                        .then_inc(s["hg_done"], 1)

                wait("moeTT_ps", 1)
                eng.tensor_tensor(src2[:, :, :], mis.rearrange("p (t d) -> p t d", t=T), src2[:, :, :], ALU.add)\
                    .then_inc(s["final_ready"], 1)
                wait("final_ready", 2)
                eng.tensor_scalar(attn[:, :, :, :].rearrange("p t h d -> p t (h d)"), src2[:, :, :], -87.0, None, ALU.max)\
                    .then_inc(s["silu_in"], 1)
                for tick in range(CUT):
                    finish(b, tick)
                    if more:
                        step(b + 1, tick, True)
                assert links[0] == NLINK or not more, links[0]

            for at in range(XN):
                front(0, at)
            eng.wait_ge(s["memset_done"], 3)
            eng.wait_ge(s["half_set"], 4)
            eng.wait_ge(s["w_in"], NW)
            eng.wait_ge(s["setup_pe"], 1)
            setup(eng.tensor_copy(WoT[:, :, :], ps_turn[:, 0, 0:2 * P].rearrange("p (c n) -> p c n", c=2)))
            setup(eng.tensor_copy(w_hi, ps_turn[:, 1, 0:2 * RF]))
            setup(eng.tensor_copy(k_hi4[0:RF, 0, 0, :], key_table))
            setup(eng.tensor_copy(pick[:, :], pick32))
            eng.wait_ge(s["setup_dve"], 4)
            setup(eng.tensor_tensor(w_lo, ps_turn[:, 1, 0:2 * RF], w_hi.bitcast(F32), ALU.subtract))
            setup(eng.tensor_tensor(k_lo4[0:RF, 0, 0, :], key_table, k_hi4[0:RF, 0, 0, :].bitcast(F32),
                                  ALU.subtract))
            eng.wait_ge(s["setup_dve"], 6)
            for i in range(1, USLOTS * QH):
                eng.tensor_copy(k_hi4[0:RF, i // QH, i % QH, :], k_hi4[0:RF, 0, 0, :].bitcast(F32))
            eng.wait_ge(s["setup_pe"], 2)
            setup(eng.tensor_copy(wqk[:, :], ps_score[:, 0, 0:P]))
            setup(eng.tensor_copy(wvo[:, 0:P], ps_score[:, 1, 0:P]))
            setup(eng.tensor_copy(y_bias[:, :], ps_guard[:, 0, 0:1]))
            setup(eng.tensor_copy(wvo[:, P:P + 1], ps_guard[:, 1, 0:1]))
            setup(eng.tensor_copy(bqbk[:, :], mis[:, 0:1]))
            setup(eng.tensor_tensor(out_bias[:, :], acc[:, 0:P], bo_row, ALU.add))
            eng.wait_ge(s["setup_dve"], 12)
            eng.memset(carrier[:, :], 0.0).then_inc(s["batch_done"], 1)
            eng.memset(rhead[:, :, :], 0.0).then_inc(s["stored"], 16)
            eng.memset(rmain[:, :], 0.0).then_inc(s["final_ready"], 1)

            for at in range(XN, MG2 + 1):
                if at == QK:
                    for c in range(NC):
                        eng.wait_ge(s["weights_hi"], NC + c + 1)
                        e = slice(CE * c, CE * c + CE)
                        eng.tensor_tensor(vals_low_stage[:, c, :], prob[:, c, :],
                                          vals_hi[:, e, :].bitcast(F32).rearrange("p e h -> p (e h)"), ALU.subtract)\
                            .then_inc(s["vals_split"], 1)
                front(0, at)
            for e in range(E):
                beside(0, e, alone=True)
            for tick in range(CUT):
                step(0, tick, True)
            assert links[0] == FLINK, links[0]
            with eng.Fori(0, B - 1) as b:
                batch(b, True)
            batch(B - 1, False)

        @block.scalar
        def _(eng):
            def front(b, at):
                def wait(name, k):
                    eng.wait_ge(s[name], b * per[name] + k)

                if at == XN:
                    wait("xnT_ps", 1)
                    eng.activation(xnT[:, :], ps_turn[:, 0, :], ACT.Copy).then_inc(s["xnT_ready"], 1)
                if at == Y:
                    wait("proj_ps", 1)
                    eng.activation(yT[:, :], ps_turn[:, 0, :], ACT.Identity, bias=y_bias[:, 0:1])\
                        .then_inc(s["y_ready"], 1)
                if at == QK:
                    for n, hi in enumerate((q_hi, k_hi)):
                        wait("proj_ps", n + 4)
                        eng.activation(hi, ps_turn[:, n, :], ACT.Copy).then_inc(s["proj_hi"], 1)

            def upper(b, h):
                def wait(name, k):
                    eng.wait_ge(s[name], b * per[name] + k)

                q = h // QH
                wait("u_sum", h + 1)
                if q >= USLOTS:
                    wait("score_ps", T + NT1 * (q - USLOTS + 1))
                eng.activation(u_hi[0:RF, q % USLOTS, h % QH, :], rot_a[0:RF, h % 2, :], ACT.Copy)\
                    .then_inc(s["u_hi_done"], 1)

            def row_max(b, q):
                def wait(name, k):
                    eng.wait_ge(s[name], b * per[name] + k)

                wait("maxT_ps", q + 1)
                if q >= 2:
                    wait("row_in", 16 * (q - 1))
                eng.activation(rowmaxT[:, q % 2, :], mis[0:QH * T, 0:P], ACT.Copy, scale=-1.0)\
                    .then_inc(s["maxT_done"], 1)

            def beside(b, e):
                def wait(name, k):
                    eng.wait_ge(s[name], b * per[name] + k)

                if e == MAIN_ROW:
                    wait("mmaxT_ps", 1)
                    eng.activation(mainrowT[:, :], mis[0:T, 0:P], ACT.Copy).then_inc(s["mmaxT_done"], 1)
                p = e - QUAD_AT
                if p >= 4 and p % 4 == 0 and p // 4 <= QH:
                    upper(b, p // 4 - 1)
                if p - 6 == NT1:
                    row_max(b, 0)

            def batch(b, more):
                def wait(name, k):
                    eng.wait_ge(s[name], b * per[name] + k)

                for tick in range(TICKS):
                    for at in (XN, Y):
                        if more and tick == FRONT_AT[at] + 1:
                            front(b + 1, at)
                    if tick == KEEP:
                        wait("batch_done", 1)
                        eng.activation(xres[:, :, :], xin[:, :, :], ACT.Copy).then_inc(s["x_free"], 1)
                        eng.activation(src2[:, :, :], xn[:, :, :], ACT.Copy).then_inc(s["xn_kept"], 1)
                    if tick < PRE - QH:
                        upper(b, QH + tick)
                    m = tick - MAIN_SCORE
                    if 0 <= m < 2 * T and m % 2 == 0:
                        jb = m // 2
                        wait("score_ps", jb + 1)
                        eng.activation(prob[:, main_slot(jb), :], ps_score[:, jb % 2, :], ACT.Exp, scale=MAIN_SCALE)\
                            .then_inc(s["exp_done"], 1)
                    n = tick - SCORE_AT
                    if 0 <= n < NT:
                        m = n // 4
                        wait("score_ps", T + n + 1)
                        if n % 4 == 0:
                            wait("pv_done", T if m < 2 else T + m - 1)
                        eng.activation(prob[:, pslot(n), :], ps_score[:, bank_of(n), :], ACT.Exp, scale=HEAD_SCALE)\
                            .then_inc(s["exp_done"], 1)
                    if (tick - TURN_AT) % 4 == 2 and PRE <= (tick - TURN_AT) // 4 < H:
                        upper(b, (tick - TURN_AT) // 4)
                    n = tick - GUARD_AT
                    if n % NT1 == 0 and 1 < n // NT1 <= NQ:
                        row_max(b, n // NT1 - 1)
                    n = tick - SCORE_AT - 20
                    if n >= 0 and n % 16 == 0 and n // 16 < NQ:
                        q = n // 16
                        wait("pv_done", T + T * (q + 1))
                        if q >= 1:
                            wait("oTT_ps", q)
                        eng.activation(oT[:, :], acc, ACT.Copy).then_inc(s["oT_done"], 1)

                wait("attnT_ps", 1)
                eng.activation(attnT[:, :], mis, ACT.Copy).then_inc(s["attnT_ready"], 1)
                if more:
                    front(b + 1, QK)
                wait("x2T_ready", 1)
                eng.activation(x2_hi, x2T, ACT.Copy).then_inc(s["x2_hi_done"], 1)
                wait("logit_ready", 1)
                eng.activation(sel[:, :, :], selx[:, :, :], ACT.Exp, scale=-1.0)\
                    .then_inc(s["esel_done"], 1)
                for e in range(E + 1):
                    if more and e < E:
                        beside(b + 1, e)
                    if e < E:
                        wait("hid_ps", e + 1)
                        if e >= 3:
                            wait("hid_lo_done", e - 2)
                        eng.activation(hid[:, e % 3, :], ps_score[:, e % 2, :], ACT.Relu).then_inc(s["relu_done"], 1)
                    if e == 1:
                        wait("gateT_ps", 1)
                        eng.activation(gateT[0:E, :], mis[0:E, :], ACT.Copy).then_inc(s["gateT_hi"], 1)
                    if e >= 1:
                        f = e - 1
                        wait("hg_done", f + 1)
                        if f >= 3:
                            wait("moe_done", f - 2)
                        eng.activation(hid_hi[f % 3], hid[:, f % 3, :], ACT.Copy).then_inc(s["hid_hi_done"], 1)
                wait("moe_done", E)
                eng.activation(moeT[:, :], acc, ACT.Copy).then_inc(s["moeT_ready"], 1)
                wait("silu_in", 1)
                eng.activation(oT[:, :].rearrange("p (t d) -> p t d", t=T),
                               attn[:, :, :, :].rearrange("p t h d -> p t (h d)"), ACT.Exp, scale=-1.0)\
                    .then_inc(s["esig_done"], 1)

            eng.wait_ge(s["setup_dve"], 6)
            for i in range(1, USLOTS * QH):
                tail = eng.activation(k_lo4[0:RF, i // QH, i % QH, :], k_lo4[0:RF, 0, 0, :].bitcast(F32), ACT.Copy)
            tail.then_inc(s["k_tables"], 1)
            eng.wait_ge(s["keys_in"], 16)
            for c in range(NC):
                eng.activation(keys_hi[:, CE * c:CE * c + CE, :].rearrange("p e h -> p (e h)"), prob[:, c, :], ACT.Copy)\
                    .then_inc(s["weights_hi"], 1)
            for at in range(MG2 + 1):
                if at == QK:
                    for c in range(NC):
                        if c % 2 == 0:
                            eng.wait_ge(s_vals_in[c // 2], 16)
                        eng.activation(vals_hi[:, CE * c:CE * c + CE, :].rearrange("p e h -> p (e h)"),
                                       prob[:, c, :], ACT.Copy).then_inc(s["weights_hi"], 1)
                    eng.wait_ge(s["vals_split"], NC)
                front(0, at)
            for e in range(E):
                beside(0, e)
            eng.wait_ge(s["low_spilled"], 32)
            with eng.Fori(0, B - 1) as b:
                batch(b, True)
            batch(B - 1, False)

        @block.gpsimd
        def _(eng):
            eng.memset(minus_half[:, :], -0.5).then_inc(s["half_set"], 1)
            eng.memset(eps[:, :], EPS).then_inc(s["half_set"], 1)
            eng.wait_ge(s["half_set"], 2)
            eng.memset(var_eps[:, :], 0.0).then_inc(s["scaled"], 1)
            eng.wait_ge(s["scaled"], 1)
            eng.memset(k_hi4[96:P, :, :, :].bitcast(F32), 1.0).then_inc(s["half_set"], 1)
            eng.wait_ge(s["half_set"], 3)
            eng.memset(k_lo4[96:P, :, :, :].bitcast(F32), 0.0).then_inc(s["half_set"], 1)
            eng.wait_ge(s["half_set"], 4)

            def root(b, side, n):
                def wait(name, k):
                    eng.wait_ge(s[name], b * per[name] + k)

                wait(side + "var_ready", n)
                eng.tensor_tensor(var_eps[:, :], mv[:, :, 1], eps[:, :], ALU.add).then_inc(s[side + "var_eps"], 1)
                wait(side + "var_eps", n)
                eng.tensor_tensor(rstd[:, :], var_eps[:, :], minus_half[:, :], ALU.pow)\
                   .then_inc(s[side + "rstd_ready"], 1)

            def add(b, h):
                eng.wait_ge(s["rot_done"], b * per["rot_done"] + 2 * h + 2)
                eng.tensor_tensor(rot_a[0:RF, h % 2, :], rot_a[0:RF, h % 2, :], rot_b[0:RF, h % 2, :], ALU.add)\
                   .then_inc(s["u_sum"], 1)

            def low(b, h):
                def wait(name, k):
                    eng.wait_ge(s[name], b * per[name] + k)

                q = h // QH
                wait("u_hi_done", h + 1)
                if q >= USLOTS:
                    wait("score_ps", T + NT1 * (q - USLOTS + 1))
                eng.tensor_tensor(u_lo[0:RF, q % USLOTS, h % QH, :], rot_a[0:RF, h % 2, :],
                                  u_hi[0:RF, q % USLOTS, h % QH, :].bitcast(F32), ALU.subtract)\
                   .then_inc(s["u_lo_done"], 1)

            def beside(b, e):
                p = e - QUAD_AT
                if p >= 4 and p % 4 == 1 and p // 4 <= QH:
                    low(b, p // 4 - 1)
                if p >= 0 and p % 4 == 2 and p // 4 < PRE:
                    add(b, p // 4)

            def head(b, h):
                if PRE <= h + 1 < H:
                    add(b, h + 1)
                low(b, h)

            def batch(b, more):
                def wait(name, k):
                    eng.wait_ge(s[name], b * per[name] + k)

                for h in range(HCUT, H):
                    head(b, h)
                if more:
                    root(b + 1, "f", 1)
                    root(b + 1, "f", 2)
                root(b, "b", 1)
                wait("x2_hi_done", 1)
                eng.tensor_tensor(x2_lo, x2T, x2_hi.bitcast(F32), ALU.subtract).then_inc(s["x2_lo_done"], 1)
                for e in range(E):
                    if more:
                        beside(b + 1, e)
                    wait("hid_hi_done", e + 1)
                    if e >= 3:
                        wait("moe_done", e - 2)
                    eng.tensor_tensor(hid_lo[e % 3], hid[:, e % 3, :], hid_hi[e % 3].bitcast(F32), ALU.subtract)\
                       .then_inc(s["hid_lo_done"], 1)
                wait("silu_in", 1)
                eng.tensor_tensor(src2[:, :, :], src2[:, :, :], smain[:, :, :], ALU.mult).then_inc(s["scaled"], 1)
                for h in range(QH, HCUT):
                    if more:
                        head(b + 1, h)
                    if h == MULTIPLY:
                        wait("inverted", T)
                        wait("scaled", 2)
                        eng.tensor_tensor(res[:, :, :], src2[:, :, :], res[:, :, :], ALU.mult)\
                           .then_inc(s["multiplied"], 1)
                    if h == ADD:
                        wait("multiplied", 1)
                        eng.tensor_tensor(res[:, :, :], res[:, :, :], xres[:, :, :], ALU.add).then_inc(s["batch_done"], 1)

            root(0, "f", 1)
            root(0, "f", 2)
            for c in range(NC):
                eng.wait_ge(s["weights_hi"], c + 1)
                e = slice(CE * c, CE * c + CE)
                eng.tensor_tensor(keys_low_stage[:, c, :], prob[:, c, :],
                                  keys_hi[:, e, :].bitcast(F32).rearrange("p e h -> p (e h)"), ALU.subtract)\
                   .then_inc(s["weights_lo"], 1)
            for e in range(E):
                beside(0, e)
            for h in range(QH, HCUT):
                head(0, h)
            with eng.Fori(0, B - 1) as b:
                batch(b, True)
            batch(B - 1, False)


_INS = ['L0_attn_hidden_states', 'L0_attn_Wq', 'L0_attn_bq', 'L0_attn_Wk', 'L0_attn_bk', 'L0_attn_Wv', 'L0_attn_bv',
        'L0_attn_Wo', 'L0_attn_bo', 'L0_ffn_wq', 'L0_ffn_wk', 'L0_ffn_wv', 'L0_ffn_wp', 'L0_ffn_wo', 'L0_ffn_ln1_g',
        'L0_ffn_ln1_b', 'L0_ffn_ln2_g', 'L0_ffn_ln2_b', 'L0_ffn_sel_w', 'L0_ffn_keys', 'L0_ffn_values']
_CONSTS = ["c_span", "c_cos", "c_sin", "c_key", "c_ident", "c_pick", "c_iota"]


def kernel(**inputs):
    import numpy as _np
    import concourse.bacc as _bacc
    from concourse import mybir as _mybir
    from concourse.bass_utils import run_bass_kernel_spmd as _run

    nc = _bacc.Bacc("TRN2", target_bir_lowering=False, num_devices=1)
    arrays, args = {}, []
    tables = position_constants()
    for name in _INS + _CONSTS:
        a = _np.ascontiguousarray(inputs[name] if name in inputs else tables[name])
        arrays[f"in_{name}_dram"] = a
        args.append(nc.dram_tensor(f"in_{name}_dram", a.shape, _mybir.dt.from_np(a.dtype), kind="ExternalInput").ap())
    args.append(nc.dram_tensor("out_0_dram", (B, S, P), F32, kind="ExternalOutput").ap())
    build(nc, *args)
    r = _run(nc, [arrays], core_ids=[0])
    return r.results[0]["out_0_dram"]
```
